# Optimizing a Trainium2 kernel written in Bass

```python
import numpy as np
import jax
import jax.numpy as jnp

def _softmax(x, axis=-1):
    return jax.nn.softmax(x, axis=axis)

def _gelu(x):
    return jax.nn.gelu(x, approximate=True)

def _silu(x):
    return jax.nn.silu(x)

def _sigmoid(x):
    return jax.nn.sigmoid(x)

def _layernorm(x, axis=-1, eps=1e-05):
    m = jnp.mean(x, axis=axis, keepdims=True)
    v = jnp.var(x, axis=axis, keepdims=True)
    return (x - m) / jnp.sqrt(v + eps)

def _scatter_add(tgt, idx, src, axis=0):
    return tgt.at[idx].add(src)

def _segment_sum(src, seg, n):
    return jax.ops.segment_sum(src, seg, n)
kernel_name = 'mk_conv_attn_hybrid_d2_conv_nchw128_r4_524494'

def setup_inputs(seed: int=0):
    np.random.seed(seed)
    _w = jnp.asarray

    def _rec_inputs():
        import jax
        import jax.numpy as jnp
        _gk = jax.random.key(seed)
        x = -0.0002928 + 1 * jax.random.normal(jax.random.fold_in(_gk, 1), (8, 32, 16, 16), jnp.float32)
        return x
    x = _rec_inputs()

    def _L0_conv_setup():
        import jax, jax.numpy as jnp
        from jax import lax
        import numpy as np
        K = 3
        STRIDE = 1
        PAD = 1
        DIL = 1

        def _deform_conv(x, w_off, b_off, w_dcn):
            B, C, H, W = x.shape
            Ho = (H + 2 * PAD - DIL * (K - 1) - 1) // STRIDE + 1
            Wo = (W + 2 * PAD - DIL * (K - 1) - 1) // STRIDE + 1
            KK = K * K
            offset = lax.conv_general_dilated(x, w_off, window_strides=(STRIDE, STRIDE), padding=[(PAD, PAD), (PAD, PAD)], rhs_dilation=(DIL, DIL), dimension_numbers=('NCHW', 'OIHW', 'NCHW'))
            offset = offset + b_off[None, :, None, None]
            off = offset.reshape(B, KK, 2, Ho, Wo)
            dy, dx = (off[:, :, 0], off[:, :, 1])
            ky, kx = jnp.meshgrid(jnp.arange(K), jnp.arange(K), indexing='ij')
            ky = (ky.reshape(-1) * DIL).astype(x.dtype)
            kx = (kx.reshape(-1) * DIL).astype(x.dtype)
            base_y = (jnp.arange(Ho) * STRIDE - PAD).astype(x.dtype)[None, :, None] + ky[:, None, None]
            base_x = (jnp.arange(Wo) * STRIDE - PAD).astype(x.dtype)[None, None, :] + kx[:, None, None]
            y = base_y[None] + dy
            xc = base_x[None] + dx
            y0 = jnp.floor(y)
            x0 = jnp.floor(xc)
            wy = y - y0
            wx = xc - x0
            y0i = y0.astype(jnp.int32)
            x0i = x0.astype(jnp.int32)

            def sample_one(xb, y0i, x0i, wy, wx):
                xf = xb.reshape(C, H * W)

                def corner(iy, ix):
                    valid = (iy >= 0) & (iy < H) & (ix >= 0) & (ix < W)
                    idx = jnp.clip(iy, 0, H - 1) * W + jnp.clip(ix, 0, W - 1)
                    v = jnp.take(xf, idx.reshape(-1), axis=1).reshape(C, KK, Ho, Wo)
                    return v * valid[None].astype(xb.dtype)
                v00 = corner(y0i, x0i)
                v01 = corner(y0i, x0i + 1)
                v10 = corner(y0i + 1, x0i)
                v11 = corner(y0i + 1, x0i + 1)
                return v00 * (1 - wy) * (1 - wx) + v01 * (1 - wy) * wx + v10 * wy * (1 - wx) + v11 * wy * wx
            sampled = jax.vmap(sample_one)(x, y0i, x0i, wy, wx)
            w = w_dcn.reshape(w_dcn.shape[0], C, KK)
            return jnp.einsum('bckhw,ock->bohw', sampled, w)
        key = jax.random.key(seed)
        k1, k2, k3, k4 = jax.random.split(key, 4)
        B, C, H, W, Co = (8, 32, 16, 16, 32)
        x = jax.random.normal(k1, (B, C, H, W), jnp.float32)
        w_off = jax.random.normal(k2, (2 * K * K, C, K, K), jnp.float32) * 0.01
        b_off = jax.random.normal(k3, (2 * K * K,), jnp.float32) * 0.01
        w_dcn = jax.random.normal(k4, (Co, C, K, K), jnp.float32) * (1.0 / np.sqrt(C * K * K))
        return {'x': x, 'w_off': w_off, 'b_off': b_off, 'w_dcn': w_dcn}
    _L0_conv_all = _L0_conv_setup()
    _L0_conv_in = {k: v for k, v in _L0_conv_all.items() if k in ('w_off', 'b_off', 'w_dcn')}
    del _L0_conv_all

    def _L1_attn_setup():
        import jax, jax.numpy as jnp
        import numpy as np
        B, N, D = (8, 512, 32)
        N_LAYER, N_HEAD = (4, 8)
        PARAMS_STD = 0.05

        def _attention(V, Q, Z):
            n = Z.shape[1]
            Attn = jnp.einsum('bni,ij,bmj->bnm', Z, Q, Z)
            values = jnp.einsum('ij,bnj->bni', V, Z)
            return jnp.einsum('bnm,bmi->bni', Attn, values) / n
        key = jax.random.key(seed)
        kz, kv, kq = jax.random.split(key, 3)
        Z = jax.random.normal(kz, (B, N, D), dtype=jnp.float32)
        v_matrix = PARAMS_STD * jax.random.normal(kv, (N_LAYER, N_HEAD, 1, D, D), dtype=jnp.float32)
        q_matrix = PARAMS_STD * jax.random.normal(kq, (N_LAYER, N_HEAD, 1, D, D), dtype=jnp.float32)
        return {'Z': Z, 'v_matrix': v_matrix, 'q_matrix': q_matrix}
    _L1_attn_all = _L1_attn_setup()
    _L1_attn_in = {k: v for k, v in _L1_attn_all.items() if k in ('v_matrix', 'q_matrix')}
    del _L1_attn_all

    def _L1_ffn_setup():
        import jax, jax.numpy as jnp
        import numpy as np
        B, S, D, E, H, O, K = (128, 512, 32, 16, 128, 32, 8)
        key = jax.random.key(seed)
        k0, k1, k2, k3 = jax.random.split(key, 4)
        x = jax.random.normal(k0, (B, S, D), dtype=jnp.float32)
        gate_w = jax.random.normal(k1, (E, D), dtype=jnp.float32) * (1.0 / np.sqrt(D))
        gate_b = jnp.zeros((E,), dtype=jnp.float32)
        weight1 = jax.random.uniform(k2, (E, D + 1, H), dtype=jnp.float32, minval=-1.0, maxval=1.0) * (1.0 / np.sqrt(D + 1))
        weight2 = jax.random.uniform(k3, (E, H + 1, O), dtype=jnp.float32, minval=-1.0, maxval=1.0) * (1.0 / np.sqrt(H + 1))
        return {'x': x, 'gate_w': gate_w, 'gate_b': gate_b, 'weight1': weight1, 'weight2': weight2}
    _L1_ffn_all = _L1_ffn_setup()
    _L1_ffn_in = {k: v for k, v in _L1_ffn_all.items() if k in ('gate_w', 'gate_b', 'weight1', 'weight2')}
    del _L1_ffn_all
    return {'x': x, 'L0_conv_w_off': _L0_conv_in['w_off'], 'L0_conv_b_off': _L0_conv_in['b_off'], 'L0_conv_w_dcn': _L0_conv_in['w_dcn'], 'L1_attn_v_matrix': _L1_attn_in['v_matrix'], 'L1_attn_q_matrix': _L1_attn_in['q_matrix'], 'L1_ffn_gate_w': _L1_ffn_in['gate_w'], 'L1_ffn_gate_b': _L1_ffn_in['gate_b'], 'L1_ffn_weight1': _L1_ffn_in['weight1'], 'L1_ffn_weight2': _L1_ffn_in['weight2']}

def reference(x, L0_conv_w_off, L0_conv_b_off, L0_conv_w_dcn, L1_attn_v_matrix, L1_attn_q_matrix, L1_ffn_gate_w, L1_ffn_gate_b, L1_ffn_weight1, L1_ffn_weight2):
    import jax
    import jax.numpy as jnp

    def _L0_conv_ref(x, w_off, b_off, w_dcn):
        import jax, jax.numpy as jnp
        from jax import lax
        import numpy as np
        K = 3
        STRIDE = 1
        PAD = 1
        DIL = 1

        def _deform_conv(x, w_off, b_off, w_dcn):
            B, C, H, W = x.shape
            Ho = (H + 2 * PAD - DIL * (K - 1) - 1) // STRIDE + 1
            Wo = (W + 2 * PAD - DIL * (K - 1) - 1) // STRIDE + 1
            KK = K * K
            offset = lax.conv_general_dilated(x, w_off, window_strides=(STRIDE, STRIDE), padding=[(PAD, PAD), (PAD, PAD)], rhs_dilation=(DIL, DIL), dimension_numbers=('NCHW', 'OIHW', 'NCHW'))
            offset = offset + b_off[None, :, None, None]
            off = offset.reshape(B, KK, 2, Ho, Wo)
            dy, dx = (off[:, :, 0], off[:, :, 1])
            ky, kx = jnp.meshgrid(jnp.arange(K), jnp.arange(K), indexing='ij')
            ky = (ky.reshape(-1) * DIL).astype(x.dtype)
            kx = (kx.reshape(-1) * DIL).astype(x.dtype)
            base_y = (jnp.arange(Ho) * STRIDE - PAD).astype(x.dtype)[None, :, None] + ky[:, None, None]
            base_x = (jnp.arange(Wo) * STRIDE - PAD).astype(x.dtype)[None, None, :] + kx[:, None, None]
            y = base_y[None] + dy
            xc = base_x[None] + dx
            y0 = jnp.floor(y)
            x0 = jnp.floor(xc)
            wy = y - y0
            wx = xc - x0
            y0i = y0.astype(jnp.int32)
            x0i = x0.astype(jnp.int32)

            def sample_one(xb, y0i, x0i, wy, wx):
                xf = xb.reshape(C, H * W)

                def corner(iy, ix):
                    valid = (iy >= 0) & (iy < H) & (ix >= 0) & (ix < W)
                    idx = jnp.clip(iy, 0, H - 1) * W + jnp.clip(ix, 0, W - 1)
                    v = jnp.take(xf, idx.reshape(-1), axis=1).reshape(C, KK, Ho, Wo)
                    return v * valid[None].astype(xb.dtype)
                v00 = corner(y0i, x0i)
                v01 = corner(y0i, x0i + 1)
                v10 = corner(y0i + 1, x0i)
                v11 = corner(y0i + 1, x0i + 1)
                return v00 * (1 - wy) * (1 - wx) + v01 * (1 - wy) * wx + v10 * wy * (1 - wx) + v11 * wy * wx
            sampled = jax.vmap(sample_one)(x, y0i, x0i, wy, wx)
            w = w_dcn.reshape(w_dcn.shape[0], C, KK)
            return jnp.einsum('bckhw,ock->bohw', sampled, w)
        return _deform_conv(x, w_off, b_off, w_dcn)

    def _L1_attn_ref(Z, v_matrix, q_matrix):
        import jax, jax.numpy as jnp
        import numpy as np
        B, N, D = (8, 512, 32)
        N_LAYER, N_HEAD = (4, 8)
        PARAMS_STD = 0.05

        def _attention(V, Q, Z):
            n = Z.shape[1]
            Attn = jnp.einsum('bni,ij,bmj->bnm', Z, Q, Z)
            values = jnp.einsum('ij,bnj->bni', V, Z)
            return jnp.einsum('bnm,bmi->bni', Attn, values) / n
        n_layer, n_head = (v_matrix.shape[0], v_matrix.shape[1])
        for i in range(n_layer):
            Zi = Z
            residues = jnp.zeros_like(Zi)
            for j in range(n_head):
                Vij = v_matrix[i, j, 0]
                Qij = q_matrix[i, j, 0]
                residues = residues + _attention(Vij, Qij, Zi)
            Z = Zi + residues / n_head
        return Z

    def _L1_ffn_ref(x, gate_w, gate_b, weight1, weight2):
        import jax, jax.numpy as jnp
        import numpy as np
        B, S, D, E, H, O, K = (128, 512, 32, 16, 128, 32, 8)
        Bn, Sn, Dn = x.shape
        logits = jnp.einsum('bsd,ed->bse', x, gate_w) + gate_b
        probs = jax.nn.softmax(logits, axis=1)
        vals, idx = jax.lax.top_k(probs.transpose(0, 2, 1), K)
        topv = vals.transpose(0, 2, 1)
        topi = idx.transpose(0, 2, 1)
        flat_idx = topi.reshape(Bn, K * E)
        gathered = jnp.take_along_axis(x, flat_idx[:, :, None], axis=1)
        gathered = gathered.reshape(Bn, K, E, Dn)
        pooled = jnp.einsum('bked,bke->bed', gathered, topv)
        ones = jnp.ones((E, Bn, 1), dtype=x.dtype)
        h = jnp.concatenate([pooled.transpose(1, 0, 2), ones], axis=-1)
        h = jax.nn.gelu(jnp.einsum('ebd,edh->ebh', h, weight1), approximate=False)
        h = jnp.concatenate([h, ones], axis=-1)
        out = jnp.einsum('ebh,eho->ebo', h, weight2)
        out = out.transpose(1, 0, 2)
        weighted = jnp.einsum('beo,bke->bkeo', out, topv).reshape(Bn, K * E, O)
        outputs = jnp.zeros((Bn, Sn, O), dtype=x.dtype)
        outputs = outputs.at[jnp.arange(Bn)[:, None], flat_idx].add(weighted)
        return outputs

    def _gn(v, G=32, eps=1e-05):
        B_, C_, H_, W_ = v.shape
        g = v.reshape(B_, G, C_ // G, H_, W_)
        m = jnp.mean(g, axis=(2, 3, 4), keepdims=True)
        s = jnp.var(g, axis=(2, 3, 4), keepdims=True)
        return ((g - m) / jnp.sqrt(s + eps)).reshape(v.shape)

    def _ln_c(v, eps=1e-06):
        m = jnp.mean(v, axis=1, keepdims=True)
        s = jnp.var(v, axis=1, keepdims=True)
        return (v - m) / jnp.sqrt(s + eps)

    def _ln_t(v, eps=1e-05):
        m = jnp.mean(v, axis=-1, keepdims=True)
        s = jnp.var(v, axis=-1, keepdims=True)
        return (v - m) / jnp.sqrt(s + eps)

    def _to_tokens(v):
        B_, C_, H_, W_ = v.shape
        return v.reshape(B_, C_, H_ * W_).transpose(0, 2, 1)

    def _from_tokens(t, like):
        B_, C_, H_, W_ = like.shape
        return t.transpose(0, 2, 1).reshape(B_, C_, H_, W_)
    x = x + _L0_conv_ref(_gn(x), L0_conv_w_off, L0_conv_b_off, L0_conv_w_dcn)
    t = _to_tokens(x)
    t = t + _L1_attn_ref(_ln_t(t), L1_attn_v_matrix, L1_attn_q_matrix)
    t = t + _L1_ffn_ref(_ln_t(t), L1_ffn_gate_w, L1_ffn_gate_b, L1_ffn_weight1, L1_ffn_weight2)
    x = _from_tokens(t, x)
    return x

_drawn_inputs = setup_inputs


def setup_inputs(seed=0):
    import zlib

    import numpy as np

    out = dict(_drawn_inputs(seed))
    spreads = {'L1_ffn_gate_b': (0.0, 0.8)}
    factors = {'L0_conv_b_off': 4.851, 'L1_ffn_gate_w': 8.0, 'L1_ffn_weight1': 8.0, 'L1_ffn_weight2': 8.0}
    for name, (base, spread) in spreads.items():
        noise = np.random.default_rng([zlib.crc32(name.encode()), seed]).standard_normal(out[name].shape)
        drawn = base * np.exp(spread * noise) if base else spread * noise
        out[name] = jnp.asarray(drawn.astype(out[name].dtype))
    for name, factor in factors.items():
        out[name] = (out[name] * factor).astype(out[name].dtype)
    return out
```

```python
from contextlib import ExitStack

import numpy as np

import concourse.bass as bass
from concourse import mybir

F32 = mybir.dt.float32
ACT = mybir.ActivationFunctionType
ALU = mybir.AluOpType
AX = mybir.AxisListType

B, C, H, W = 8, 32, 16, 16
T = H * W
TAPS, KS = 9, 3
LAYERS, HEADS = 4, 8
E, HID, TOPK = 16, 128, 8
GN_EPS = LN_EPS = 1e-5

P = 128
GB = P // C
G = B // GB
PAIRS = GB // 2
BR = 4
BLOCKS = H // BR
BP = BR * W
UNITS = PAIRS * BLOCKS
WR = P // W
DENSE_ROWS = (0, WR)
LOCAL_ROWS = tuple(min(max(BR * j - 2, 0), H - WR) for j in range(BLOCKS))
NW = len(LOCAL_ROWS)
OC = 2 * TAPS
RING = 3


def constants():
    p = np.arange(P)
    img, ch = p // C, p % C
    t = {}
    t["identity"] = np.eye(P)
    t["same_image"] = (img[:, None] == img[None, :])
    sel = np.zeros((P, GB, OC))
    for b in range(GB):
        sel[b * OC + np.arange(OC), b, np.arange(OC)] = 1
    t["pick_offsets"] = sel
    row_in_block, col = (p % BP) // W, p % W
    k = np.arange(TAPS)
    x = col[:, None] + (k % KS - 1)[None]
    t["dx_base"] = x[:, :, None] - np.arange(W)
    y = row_in_block[:, None, None] + BR * np.arange(BLOCKS)[None, :, None] + (k // KS - 1)[None, None]
    t["dy_local"] = y[..., None] - (np.array(LOCAL_ROWS)[None, :, None, None] + np.arange(WR))
    t["dy_dense"] = y[..., None] - np.arange(H)
    t["layer_identity"] = (ch[:, None] == np.arange(C))
    t["image_expert"] = np.repeat(img[:, None] == np.arange(GB), E, axis=1)
    t["spread"] = (ch[:, None] == ch[None, :])
    t["quarter"] = (img[:, None] == np.arange(GB))
    t["own_expert"] = (p % E)[:, None] == np.arange(E)
    t["own_image"] = (p // E % GB)[:, None] == np.arange(GB)
    t["expert_columns"] = np.zeros((P, P))
    t["expert_columns"][:E] = np.arange(E)[:, None] == (p % E)[None]
    return {n: np.ascontiguousarray(a.reshape(P, -1).astype(np.float32)) for n, a in t.items()}


FIRST = ("identity", "pick_offsets")


def build(nc, ap, modes=("dense", "dense")):
    consts = constants()
    first_w = sum(consts[n].shape[1] for n in FIRST)
    all_w = sum(a.shape[1] for a in consts.values())
    with ExitStack() as ctx:
        def sb(name, shape):
            return ctx.enter_context(nc.sbuf_tensor(name, shape, F32))

        def sem(name):
            return ctx.enter_context(nc.semaphore(name))

        table = sb("table", [P, all_w])
        at = {}
        o = 0
        for n in list(FIRST) + [n for n in consts if n not in FIRST]:
            at[n] = table[:, o:o + consts[n].shape[1]]
            o += consts[n].shape[1]
        ident = at["identity"]
        same_image3 = at["same_image"].rearrange("p (b c) -> p b c", b=GB)
        x_in = [sb(f"x_in{g}", [P, T]) for g in range(G)]
        w_off = sb("w_off", [P, TAPS, GB * OC])
        b_off = sb("b_off", [P, 1])
        w_k47 = sb("w_k47", [P, 2, C])
        w_k8 = sb("w_k8", [P, P])
        q_t = sb("q_t", [P, LAYERS, HEADS * C])
        v_t = sb("v_t", [P, LAYERS, HEADS, C])
        gate_w = sb("gate_w", [P, GB * E])
        gate_b = sb("gate_b", [P, 1])
        w1 = sb("w1", [P, E // 4, HID])
        b1 = sb("b1", [E, HID])
        w2 = sb("w2", [P, E, C])
        b2 = sb("b2", [P, C])
        gn_stats = sb("gn_stats", [P, G, 6])
        gn_mv = sb("gn_mv", [P, G, 2])
        gn_r = sb("gn_r", [P, G, 5])
        gn_pad = [sb(f"gn_pad{g}", [P, H + 2, W + 2]) for g in range(G)]
        gn = [sb(f"gn{g}", [P, T]) for g in range(G)]
        gn_t = [sb(f"gn_t{g}", [P, NW, P]) for g in range(G)]
        off = [sb(f"off{g}", [GB * OC, T]) for g in range(G)]
        off_t = [sb(f"off_t{g}", [P, UNITS, TAPS, 2]) for g in range(G)]
        hat_y = sb("hat_y", [P, 2, BLOCKS * TAPS * H])
        hat_x = sb("hat_x", [P, 2, BLOCKS * TAPS * W])
        hats = sb("hats", [P, 2, TAPS * T])
        wts = sb("wts", [P, 2, BLOCKS * TAPS * 2 * P])
        samp = sb("samp", [P, 2, 2, T])
        samp8 = sb("samp8", [P, T])
        x1 = [sb(f"x1_{g}", [P, T]) for g in range(G)]
        ln_c = [sb(f"ln_c{g}", [P, T]) for g in range(G)]
        ln_sq = [sb(f"ln_sq{g}", [P, T]) for g in range(G)]
        ln_s = [sb(f"ln_s{g}", [P, 2, 7, 2 * GB]) for g in range(G)]
        z_t = [[sb(f"z_t{n}_{g}", [P, 2, P]) for g in range(G)] for n in range(2)]
        z = [[sb(f"z{n}_{g}", [P, T]) for g in range(G)] for n in range(2)]
        gram = [sb(f"gram{g}", [P, P]) for g in range(G)]
        qg = [sb(f"qg{g}", [P, HEADS * C]) for g in range(G)]
        step = [sb(f"step{g}", [P, C]) for g in range(G)]
        step_d = [sb(f"step_d{g}", [P, P]) for g in range(G)]
        ga_m = [sb(f"ga_m{g}", [P, 2, C]) for g in range(G)]
        map_d = [sb(f"map_d{g}", [P, P]) for g in range(G)]
        x2 = [sb(f"x2_{g}", [P, T]) for g in range(G)]
        logit = sb("logit", [P, T])
        logit_r = sb("logit_r", [P, T])
        top = sb("top", [P, TOPK])
        neg_max = sb("neg_max", [P, 1])
        prob = sb("prob", [P, T])
        prob_s = sb("prob_s", [P, 2])
        chosen = sb("chosen", [P, T])
        route = sb("route", [P, T])
        route_t = sb("route_t", [P, 2, P])
        pool_d = sb("pool_d", [P, G, GB * E])
        pool_e = sb("pool_e", [P, G * GB, E])
        hid = sb("hid", [P, P])
        ex_all = sb("ex_all", [P, E, C])
        ex = sb("ex", [P, C])
        ex_b = sb("ex_b", [P, C])
        ex_d = sb("ex_d", [P, GB, C])
        y = [sb(f"y{g}", [P, T]) for g in range(G)]

        bank = [ctx.enter_context(nc.psum_tensor(f"bank{i}", [P, 512], F32)) for i in range(8)]
        ring = bank[:RING]
        smp_ps = [bank[3], bank[4]]
        s8_ps = bank[5]
        conv_ps = bank[6]
        misc = bank[7]

        s = {n: sem(n) for n in (
            "x0_in", "x1_in", "tab0_in", "tab1_in", "woff_in", "wk_in", "qv_in", "ffn_in",
            "pad_set", "gn_var", "gn_std", "gn_done", "off_mm", "off_done", "gnt_mm", "gnt_done",
            "offt_mm", "offt_done", "dist", "absd", "hat", "prod", "evac", "smp_mm", "smp_done", "co_mm", "tr_bank",
            "s8_done", "conv_mm", "x1_done",
            "ln_tr", "ln_c", "ln_sq", "ln_var", "ln_std", "zt_done", "z_tr", "z_done",
            "gram_mm", "gram_done", "qg_mm", "qg_done", "st_mm", "st_done", "std_done",
            "ga_mm", "ga_done", "gm_mm", "gm_done", "map_mm", "map_done", "att_mm", "x2_done",
            "lg_mm", "lg_done", "top_done", "prob_done", "route_done", "rt_mm", "rt_done",
            "pl_mm", "pl_done", "sp_mm", "sp_done", "hid_mm", "hid_done", "ex_mm", "ex_done",
            "y_mm", "y_done", "out_done", "dve", "act")}

        block = ctx.enter_context(nc.Block())

        def windows(mode, j):
            return (j,) if mode == "local" else (0, NW - 1)

        def wcount(g):
            return len(windows(modes[g], 0))

        def bank0(g, pr):
            per = TAPS * BLOCKS // 4
            return sum(per * PAIRS * wcount(i) for i in range(g)) + per * wcount(g) * pr

        def banks_upto(g, pr, j):
            n = TAPS * wcount(g) * (j + 1)
            return bank0(g, pr) + -(-n // 4)

        def unit(u):
            return u // UNITS, u // BLOCKS % PAIRS, u % BLOCKS

        @block.sync
        def _(sp):
            sp.dma_start(x_in[0][:], ap["x"][0]).then_inc(s["x0_in"], 16)
            sp.dma_start(table[:, :first_w], ap["table"][:, :first_w]).then_inc(s["tab0_in"], 16)
            sp.dma_start(x_in[1][:], ap["x"][1]).then_inc(s["x1_in"], 16)
            sp.dma_start(table[:, first_w:], ap["table"][:, first_w:]).then_inc(s["tab1_in"], 16)
            sp.dma_start(w_k47[:], ap["w_k47"]).then_inc(s["wk_in"], 16)
            sp.dma_start(w_k8[:], ap["w_k8"]).then_inc(s["wk_in"], 16)
            sp.dma_start(q_t[:], ap["q_t"]).then_inc(s["qv_in"], 16)
            sp.dma_start(v_t[:], ap["v_t"]).then_inc(s["qv_in"], 16)
            sp.dma_start(gate_w[:], ap["gate_w"]).then_inc(s["ffn_in"], 16)
            sp.dma_start(gate_b[:], ap["gate_b"]).then_inc(s["ffn_in"], 16)
            sp.dma_start(w1[:], ap["w1"]).then_inc(s["ffn_in"], 16)
            sp.dma_start(b1[:], ap["b1"]).then_inc(s["ffn_in"], 16)
            sp.dma_start(w2[:], ap["w2"]).then_inc(s["ffn_in"], 16)
            sp.dma_start(b2[:], ap["b2"]).then_inc(s["ffn_in"], 16)
            for g in range(G):
                sp.wait_ge(s["y_done"], g + 1)
                sp.dma_start(ap["out"][g], y[g][:]).then_inc(s["out_done"], 16)
            sp.wait_ge(s["out_done"], 16 * G)

        FFN_IN = 16 * 6

        @block.gpsimd
        def _(pool):
            for g in range(G):
                pool.memset(gn_pad[g][:], 0.0).then_inc(s["pad_set"], 1)

        @block.vector
        def _(dve):
            count = [0]

            def link(ins):
                count[0] += 1
                ins.then_inc(s["dve"], 1)
                dve.wait_ge(s["dve"], count[0])

            def newton(r, v, tmp, final, signal):
                link(dve.scalar_tensor_tensor(out=tmp, in0=r, scalar=-0.5, in1=r, op0=ALU.mult, op1=ALU.mult))
                link(dve.tensor_tensor(tmp, tmp, v, ALU.mult))
                ins = dve.scalar_tensor_tensor(out=final, in0=tmp, scalar=1.5, in1=r, op0=ALU.add, op1=ALU.mult)
                link(ins) if signal is None else ins.then_inc(signal, 1)

            def group_norm(g):
                dve.wait_ge(s["x0_in"] if g == 0 else s["x1_in"], 16)
                link(dve.bn_stats(gn_stats[:, g, :], x_in[g][:]))
                link(dve.bn_aggr(gn_mv[:, g, :], gn_stats[:, g, :]))
                r = gn_r
                dve.tensor_scalar(r[:, g, 0:1], gn_mv[:, g, 1:2], GN_EPS, None, ALU.add).then_inc(s["gn_var"], 1)
                dve.wait_ge(s["gn_var"], g + 1)
                dve.wait_ge(s["gn_std"], g + 1)
                link(dve.reciprocal(r[:, g, 2:3], r[:, g, 1:2]))
                newton(r[:, g, 2:3], r[:, g, 0:1], r[:, g, 3:4], r[:, g, 4:5], None)
                dve.wait_ge(s["pad_set"], g + 1)
                dve.tensor_scalar(gn_pad[g][:, 1:H + 1, 1:W + 1], x_in[g][:].rearrange("p (h w) -> p h w", h=H),
                                  gn_mv[:, g, 0:1], r[:, g, 4:5], ALU.subtract, ALU.mult).then_inc(s["gn_done"], 1)
                dve.tensor_scalar(gn[g][:], x_in[g][:], gn_mv[:, g, 0:1], r[:, g, 4:5], ALU.subtract,
                                  ALU.mult).then_inc(s["gn_done"], 1)

            def offsets(g):
                dve.wait_ge(s["offt_mm"], g + 1)
                dve.tensor_copy(off_t[g][:].rearrange("p u k a -> p (u k a)"),
                                misc[:, 0:UNITS * OC]).then_inc(s["offt_done"], 1)
                dve.wait_ge(s["offt_done"], g + 1)

            def distances(g, pr):
                n, rows = g * PAIRS + pr, WR if modes[g] == "local" else H
                if n == 0:
                    dve.wait_ge(s["tab1_in"], 16)
                if n >= 2:
                    dve.wait_ge(s["prod"], BLOCKS * (n - 1))
                o = off_t[g][:, pr * BLOCKS:(pr + 1) * BLOCKS]
                ty = at["dy_local" if modes[g] == "local" else "dy_dense"]
                dve.tensor_tensor(
                    hat_y[:, n % 2, 0:BLOCKS * TAPS * rows].rearrange("p (u q) -> p u q", q=rows),
                    ty.rearrange("p (u q) -> p u q", q=rows),
                    o[:, :, :, 0].rearrange("p j k -> p (j k)").unsqueeze(2).broadcast_to([P, BLOCKS * TAPS, rows]),
                    ALU.add).then_inc(s["dist"], 1)
                dve.tensor_tensor(
                    hat_x[:, n % 2].rearrange("p (j k q) -> p j k q", j=BLOCKS, k=TAPS),
                    at["dx_base"].rearrange("p (k q) -> p k q", k=TAPS).unsqueeze(1)
                    .broadcast_to([P, BLOCKS, TAPS, W]),
                    o[:, :, :, 1].unsqueeze(3).broadcast_to([P, BLOCKS, TAPS, W]),
                    ALU.add).then_inc(s["dist"], 1)

            def product(g, pr, j):
                n, rows = g * PAIRS + pr, WR if modes[g] == "local" else H
                u = n * BLOCKS + j
                if j == 0:
                    dve.wait_ge(s["hat"], 2 * (n + 1))
                if u >= 2:
                    dve.wait_ge(s["tr_bank"], banks_upto(*unit(u - 2)))
                hy = hat_y[:, n % 2, j * TAPS * rows:(j + 1) * TAPS * rows].rearrange("p (k q) -> p k q", k=TAPS)
                hx = hat_x[:, n % 2, j * TAPS * W:(j + 1) * TAPS * W].rearrange("p (k q) -> p k q", k=TAPS)
                dve.tensor_tensor(
                    hats[:, u % 2, 0:TAPS * rows * W].rearrange("p (k r q) -> p k r q", k=TAPS, q=W),
                    hy.unsqueeze(3).broadcast_to([P, TAPS, rows, W]),
                    hx.unsqueeze(2).broadcast_to([P, TAPS, rows, W]), ALU.mult).then_inc(s["prod"], 1)

            def sampled(g, pr):
                n = g * PAIRS + pr
                dve.wait_ge(s["smp_mm"], n + 1)
                if n >= 1:
                    dve.wait_ge(s["conv_mm"], 2 * n)
                for i in range(2):
                    dve.tensor_copy(samp[:, i].rearrange("p k t -> p (k t)"), smp_ps[i][:]).then_inc(s["smp_done"], 1)

            def x1_sum(g):
                dve.wait_ge(s["co_mm"], g + 1)
                dve.tensor_tensor(x1[g][:], conv_ps[:, 0:T], x_in[g][:], ALU.add).then_inc(s["x1_done"], 1)

            def layer_norm(n, g):
                i = 2 * g + n
                st = ln_s[g][:, n]
                seg = lambda a: a.rearrange("p (s c) -> p s c", c=C)
                dve.wait_ge(s["ln_tr"], i + 1)
                link(dve.tensor_reduce(st[:, 0, :], seg(misc[:, 0:T]), AX.X, ALU.add))
                dve.scalar_tensor_tensor(out=seg(ln_c[g][:]), in0=st[:, 0, :].unsqueeze(2).broadcast_to([P, 2 * GB, C]),
                                         scalar=-1.0 / C, in1=seg(misc[:, 0:T]), op0=ALU.mult,
                                         op1=ALU.add).then_inc(s["ln_c"], 1)
                dve.wait_ge(s["ln_sq"], i + 1)
                link(dve.tensor_reduce(st[:, 1, :], seg(ln_sq[g][:]), AX.X, ALU.add))
                dve.tensor_scalar(st[:, 2, :], st[:, 1, :], 1.0 / C, LN_EPS, ALU.mult, ALU.add).then_inc(s["ln_var"], 1)
                dve.wait_ge(s["ln_var"], i + 1)
                dve.wait_ge(s["ln_std"], i + 1)
                link(dve.reciprocal(st[:, 4, :], st[:, 3, :]))
                newton(st[:, 4, :], st[:, 2, :], st[:, 5, :], st[:, 6, :], None)
                dve.wait_ge(s["ln_c"], i + 1)
                dve.tensor_tensor(seg(z_t[n][g][:].rearrange("p h q -> p (h q)")), seg(ln_c[g][:]),
                                  st[:, 6, :].unsqueeze(2).broadcast_to([P, 2 * GB, C]),
                                  ALU.mult).then_inc(s["zt_done"], 1)

            def spread_diag(out, compact, signal):
                dve.tensor_tensor(out.rearrange("p (b c) -> p b c", b=GB),
                                  compact.unsqueeze(1).broadcast_to([P, GB, C]), same_image3,
                                  ALU.mult).then_inc(signal, 1)

            def gram_start(g):
                dve.wait_ge(s["gram_mm"], g + 1)
                dve.tensor_tensor(gram[g][:], misc[:, 0:P], at["same_image"], ALU.mult).then_inc(s["gram_done"], 1)
                dve.wait_ge(s["gram_done"], (LAYERS * g) + 1)

            def chain_layer(g, l):
                n = g * LAYERS + l
                dve.wait_ge(s["st_mm"], n + 1)
                dve.scalar_tensor_tensor(out=step[g][:], in0=misc[:, 256:256 + C], scalar=1.0 / (T * HEADS),
                                         in1=at["layer_identity"], op0=ALU.mult, op1=ALU.add).then_inc(s["st_done"], 1)
                dve.wait_ge(s["st_done"], n + 1)
                if l < LAYERS - 1:
                    spread_diag(step_d[g][:], step[g][:], s["std_done"])
                    dve.wait_ge(s["ga_mm"], g * (LAYERS - 1) + l + 1)
                    dve.tensor_copy(ga_m[g][:, 0], misc[:, 288:288 + C]).then_inc(s["ga_done"], 1)
                    dve.wait_ge(s["gm_mm"], g * (LAYERS - 1) + l + 1)
                    if l < LAYERS - 2:
                        link(dve.tensor_copy(ga_m[g][:, 1], misc[:, 320 + C:320 + 2 * C]))
                    else:
                        spread_diag(map_d[g][:], misc[:, 320 + C:320 + 2 * C], s["gm_done"])
                    spread_diag(gram[g][:], misc[:, 320:320 + C], s["gram_done"])
                else:
                    dve.wait_ge(s["map_mm"], g + 1)
                    spread_diag(map_d[g][:], misc[:, 288:288 + C], s["map_done"])

            def x2_sum(g):
                dve.wait_ge(s["att_mm"], g + 1)
                dve.tensor_tensor(x2[g][:], misc[:, 0:T], x1[g][:], ALU.add).then_inc(s["x2_done"], 1)

            def experts():
                dve.wait_ge(s["lg_done"], 1)
                dve.max(top[:], logit[:]).then_inc(s["top_done"], 1)
                dve.wait_ge(s["top_done"], 1)
                dve.tensor_scalar(neg_max[:], top[:, 0:1], -1.0, None, ALU.mult).then_inc(s["top_done"], 1)
                link(dve.match_replace(logit_r[:], top[:], logit[:], -3.0e38))
                link(dve.tensor_tensor(chosen[:], logit[:], logit_r[:], ALU.not_equal))
                dve.wait_ge(s["prob_done"], 1)
                link(dve.reciprocal(prob_s[:, 1:2], prob_s[:, 0:1]))
                dve.scalar_tensor_tensor(out=route[:], in0=prob[:], scalar=prob_s[:, 1:2], in1=chosen[:],
                                         op0=ALU.mult, op1=ALU.mult).then_inc(s["route_done"], 1)
                dve.wait_ge(s["rt_mm"], 1)
                dve.tensor_copy(route_t[:].rearrange("p h q -> p (h q)"), misc[:, 0:2 * P]).then_inc(s["rt_done"], 1)
                dve.wait_ge(s["pl_mm"], 1)
                dve.tensor_tensor(pool_d[:], bank[0][:, 0:P].rearrange("p (g q) -> p g q", g=G),
                                  at["image_expert"].unsqueeze(1).broadcast_to([P, G, GB * E]),
                                  ALU.mult).then_inc(s["pl_done"], 1)
                dve.wait_ge(s["sp_mm"], 1)
                dve.tensor_tensor(pool_e[:].rearrange("p i (j r) -> p (i j) r", r=4),
                                  bank[1][:, 0:P].rearrange("p (n r) -> p n r", r=4),
                                  at["quarter"].unsqueeze(1).broadcast_to([P, P // 4, 4]),
                                  ALU.mult).then_inc(s["sp_done"], 1)
                dve.wait_ge(s["ex_mm"], 1)
                link(dve.tensor_tensor(ex_all[:], bank[3][:].rearrange("p (e o) -> p e o", e=E),
                                       at["own_expert"].unsqueeze(2).broadcast_to([P, E, C]), ALU.mult))
                link(dve.tensor_reduce(ex[:], ex_all[:].rearrange("p e o -> p o e"), AX.X, ALU.add))
                link(dve.tensor_tensor(ex_b[:], ex[:], b2[:], ALU.add))
                dve.tensor_tensor(ex_d[:], ex_b[:].unsqueeze(1).broadcast_to([P, GB, C]),
                                  at["own_image"].unsqueeze(2).broadcast_to([P, GB, C]),
                                  ALU.mult).then_inc(s["ex_done"], 1)
                for g in range(G):
                    dve.wait_ge(s["y_mm"], g + 1)
                    dve.tensor_tensor(y[g][:], bank[4 + g][:, 0:T], x2[g][:], ALU.add).then_inc(s["y_done"], 1)

            for g in range(G):
                group_norm(g)
            for g in range(G):
                offsets(g)
                distances(g, 0)
                for pr in range(PAIRS):
                    if pr + 1 < PAIRS:
                        distances(g, pr + 1)
                    for j in range(BLOCKS):
                        product(g, pr, j)
                    sampled(g, pr)
                x1_sum(g)
            for g in range(G):
                layer_norm(0, g)
                gram_start(g)
                for l in range(LAYERS):
                    chain_layer(g, l)
                x2_sum(g)
                layer_norm(1, g)
            dve.wait_ge(s["ffn_in"], FFN_IN)
            experts()

        @block.scalar
        def _(act):
            act.dma_start(w_off[:], ap["w_off"]).then_inc(s["woff_in"], 16)
            act.dma_start(b_off[:], ap["b_off"]).then_inc(s["woff_in"], 16)

            def group_norm(g):
                act.wait_ge(s["gn_var"], g + 1)
                act.activation(gn_r[:, g, 1:2], gn_r[:, g, 0:1], ACT.Sqrt).then_inc(s["gn_std"], 1)

            def offsets(g):
                act.wait_ge(s["off_mm"], g + 1)
                if g == 0:
                    act.wait_ge(s["woff_in"], 32)
                act.activation(off[g][:], misc[0:GB * OC, 0:T], ACT.Identity,
                               bias=b_off[0:GB * OC, 0:1]).then_inc(s["off_done"], 1)
                act.wait_ge(s["gnt_mm"], g + 1)
                act.copy(gn_t[g][:].rearrange("p w q -> p (w q)"), conv_ps[:]).then_inc(s["gnt_done"], 1)

            def hat(g, pr):
                n, rows = g * PAIRS + pr, WR if modes[g] == "local" else H
                for a, (buf, size) in enumerate(((hat_y, BLOCKS * TAPS * rows), (hat_x, BLOCKS * TAPS * W))):
                    d = buf[:, n % 2, 0:size]
                    act.wait_ge(s["dist"], 2 * n + a + 1)
                    act.activation(d, d, ACT.Abs).then_inc(s["absd"], 1)
                    act.wait_ge(s["absd"], 2 * n + a + 1)
                    act.activation(d, d, ACT.Relu, bias=1.0, scale=-1.0).then_inc(s["hat"], 1)

            def evacuate(g, pr, i0, i1):
                n = g * PAIRS + pr
                for i in range(i0, i1):
                    f = bank0(g, pr) + i
                    act.wait_ge(s["tr_bank"], f + 1)
                    act.copy(wts[:, n % 2, 512 * i:512 * i + 512], ring[f % RING][:]).then_inc(s["evac"], 1)

            def s8(g):
                act.wait_ge(s["smp_mm"], (g + 1) * PAIRS)
                if g >= 1:
                    act.wait_ge(s["co_mm"], g)
                act.copy(samp8[:], s8_ps[:, 0:T]).then_inc(s["s8_done"], 1)

            def layer_norm(n, g):
                i = 2 * g + n
                act.wait_ge(s["ln_c"], i + 1)
                act.activation(ln_sq[g][:], ln_c[g][:], ACT.Square).then_inc(s["ln_sq"], 1)
                act.wait_ge(s["ln_var"], i + 1)
                act.activation(ln_s[g][:, n, 3, :], ln_s[g][:, n, 2, :], ACT.Sqrt).then_inc(s["ln_std"], 1)
                act.wait_ge(s["z_tr"], i + 1)
                act.copy(z[n][g][:], bank[5][:, 0:T]).then_inc(s["z_done"], 1)

            for g in range(G):
                group_norm(g)
            for g in range(G):
                offsets(g)
                per = TAPS * BLOCKS * wcount(g) // 4
                hat(g, 0)
                for pr in range(PAIRS):
                    if pr + 1 < PAIRS:
                        hat(g, pr + 1)
                    n = g * PAIRS + pr
                    if n >= 2:
                        act.wait_ge(s["smp_mm"], n - 1)
                    evacuate(g, pr, 0, per)
                s8(g)
            for g in range(G):
                layer_norm(0, g)
                for l in range(LAYERS):
                    n = g * LAYERS + l
                    act.wait_ge(s["qg_mm"], n + 1)
                    act.copy(qg[g][:], misc[:, 0:HEADS * C]).then_inc(s["qg_done"], 1)
                layer_norm(1, g)
            act.wait_ge(s["ffn_in"], FFN_IN)
            act.wait_ge(s["lg_mm"], 1)
            act.activation(logit[:], misc[:, 0:T], ACT.Identity, bias=gate_b[:, 0:1]).then_inc(s["lg_done"], 1)
            act.wait_ge(s["lg_done"], 1)
            act.wait_ge(s["top_done"], 2)
            act.activation(prob[:], logit[:], ACT.Exp, bias=neg_max[:, 0:1],
                           accum_out=prob_s[:, 0:1]).then_inc(s["prob_done"], 1)
            act.wait_ge(s["hid_mm"], 1)
            act.activation(hid[:], bank[2][:, 0:P], ACT.Gelu).then_inc(s["hid_done"], 1)

        @block.tensor
        def _(pe):
            def offsets(g):
                pe.wait_ge(s["gn_done"], 2 * g + 1)
                if g == 0:
                    pe.wait_ge(s["woff_in"], 32)
                    pe.wait_ge(s["tab0_in"], 16)
                else:
                    pe.wait_ge(s["offt_done"], g)
                for t in range(TAPS):
                    dy, dx = divmod(t, KS)
                    mm = pe.matmul(misc[0:GB * OC, 0:T], w_off[:, t, :], gn_pad[g][:, dy:dy + H, dx:dx + W],
                                   start=(t == 0), stop=(t == TAPS - 1))
                mm.then_inc(s["off_mm"], 1)
                if g:
                    pe.wait_ge(s["x1_done"], g)
                pe.wait_ge(s["gn_done"], 2 * g + 2)
                for w, r in enumerate(LOCAL_ROWS):
                    mm = pe.transpose(conv_ps[:, w * P:(w + 1) * P], gn[g][:, r * W:(r + WR) * W], ident)
                mm.then_inc(s["gnt_mm"], 1)
                pe.wait_ge(s["off_done"], g + 1)
                for pr in range(PAIRS):
                    for j in range(BLOCKS):
                        u = pr * BLOCKS + j
                        for i in range(2):
                            mm = pe.matmul(misc[i * BP:(i + 1) * BP, u * OC:(u + 1) * OC],
                                           off[g][:, j * BP:(j + 1) * BP],
                                           at["pick_offsets"][0:GB * OC, (2 * pr + i) * OC:(2 * pr + i + 1) * OC],
                                           start=True, stop=True)
                mm.then_inc(s["offt_mm"], 1)

            def transposes(g, pr, j):
                nw = wcount(g)
                u = (g * PAIRS + pr) * BLOCKS + j
                pe.wait_ge(s["prod"], u + 1)
                for i in range(TAPS * nw):
                    slot = j * TAPS * nw + i
                    f = bank0(g, pr) + slot // 4
                    if slot % 4 == 0 and f >= RING:
                        pe.wait_ge(s["evac"], f - RING + 1)
                    t, h = divmod(i, nw)
                    mm = pe.transpose(ring[f % RING][:, (slot % 4) * P:(slot % 4 + 1) * P],
                                      hats[:, u % 2, (t * nw + h) * P:(t * nw + h + 1) * P], ident)
                    if slot % 4 == 3:
                        mm.then_inc(s["tr_bank"], 1)

            def sample(g, pr, j):
                nw = wcount(g)
                n = g * PAIRS + pr
                if j == 0:
                    if n == 0:
                        pass
                    else:
                        pe.wait_ge(s["smp_done"], 2 * n)
                    if pr == 0:
                        pe.wait_ge(s["gnt_done"], g + 1)
                        if g:
                            pe.wait_ge(s["s8_done"], g)
                pe.wait_ge(s["evac"], banks_upto(g, pr, j))
                w = wts[:, n % 2, 0:BLOCKS * TAPS * nw * P].rearrange(
                    "q (j k h i p) -> q j k h i p", j=BLOCKS, k=TAPS, h=nw, i=2)
                mm = None
                for i in range(2):
                    b = 2 * pr + i
                    for h, win in enumerate(windows(modes[g], j)):
                        lhs = gn_t[g][:, win, b * C:(b + 1) * C]
                        for jj in range(4):
                            mm = pe.matmul(
                                smp_ps[i][jj * C:(jj + 1) * C, :].rearrange("p (k t) -> p k t", k=2)[:, :, j * BP:(j + 1) * BP],
                                lhs, w[:, j, jj:TAPS - 1:4, h, i, :], start=(h == 0), stop=(h == nw - 1),
                                tile_position=(0, jj * C))
                        mm = pe.matmul(s8_ps[b * C:(b + 1) * C, j * BP:(j + 1) * BP], lhs, w[:, j, TAPS - 1, h, i, :],
                                       start=(h == 0), stop=(h == nw - 1), tile_position=(0, b * C))
                if j == BLOCKS - 1:
                    mm.then_inc(s["smp_mm"], 1)

            def contract(g, pr):
                n = g * PAIRS + pr
                if n == 0:
                    pe.wait_ge(s["wk_in"], 32)
                if pr == 0:
                    pe.wait_ge(s["gnt_done"], g + 1)
                pe.wait_ge(s["smp_done"], 2 * (n + 1))
                for i in range(2):
                    b = 2 * pr + i
                    for k in range(2):
                        mm = pe.matmul(conv_ps[b * C:(b + 1) * C, 0:T], w_k47[:, k, :], samp[:, i, k, :],
                                       start=(k == 0), stop=False, tile_position=(0, b * C), skip_group_check=True)
                    mm.then_inc(s["conv_mm"], 1)

            def contract8(g):
                pe.wait_ge(s["s8_done"], g + 1)
                pe.matmul(conv_ps[:, 0:T], w_k8[:], samp8[:], start=False, stop=True,
                          skip_group_check=True).then_inc(s["co_mm"], 1)

            def layer_norm(n, g, src, done):
                i = 2 * g + n
                pe.wait_ge(s[done], g + 1)
                for h in range(2):
                    mm = pe.transpose(misc[:, h * P:(h + 1) * P], src[g][:, h * P:(h + 1) * P], ident)
                mm.then_inc(s["ln_tr"], 1)

            def z_back(n, g):
                i = 2 * g + n
                pe.wait_ge(s["zt_done"], i + 1)
                if i >= 1:
                    pe.wait_ge(s["z_done"], i)
                for h in range(2):
                    mm = pe.transpose(bank[5][:, h * P:(h + 1) * P], z_t[n][g][:, h, :], ident)
                mm.then_inc(s["z_tr"], 1)

            def gram_start(g):
                pe.wait_ge(s["zt_done"], 2 * g + 1)
                for h in range(2):
                    mm = pe.matmul(misc[:, 0:P], z_t[0][g][:, h, :], z_t[0][g][:, h, :], start=(h == 0), stop=(h == 1))
                mm.then_inc(s["gram_mm"], 1)

            def chain_layer(g, l):
                n = g * LAYERS + l
                pe.wait_ge(s["gram_done"], n + 1)
                if n == 0:
                    pe.wait_ge(s["qv_in"], 32)
                pe.matmul(misc[:, 0:HEADS * C], gram[g][:], q_t[:, l, :], start=True, stop=True).then_inc(s["qg_mm"], 1)
                pe.wait_ge(s["qg_done"], n + 1)
                for h in range(HEADS):
                    for b in range(GB):
                        r = slice(b * C, (b + 1) * C)
                        mm = pe.matmul(misc[r, 256:256 + C], qg[g][r, h * C:(h + 1) * C], v_t[r, l, h, :],
                                       start=(h == 0), stop=(h == HEADS - 1), tile_position=(b * C, b * C),
                                       skip_group_check=True)
                mm.then_inc(s["st_mm"], 1)
                pe.wait_ge(s["st_done"], n + 1)
                if l < LAYERS - 1:
                    m = g * (LAYERS - 1) + l
                    pe.matmul(misc[:, 288:288 + C], gram[g][:], step[g][:], start=True, stop=True).then_inc(s["ga_mm"], 1)
                    pe.wait_ge(s["std_done"], m + 1)
                    pe.wait_ge(s["ga_done"], m + 1)
                    pe.matmul(misc[:, 320:320 + C], step_d[g][:], ga_m[g][:, 0], start=True, stop=True)
                    mt = at["layer_identity"] if l == 0 else ga_m[g][:, 1]
                    pe.matmul(misc[:, 320 + C:320 + 2 * C], step_d[g][:], mt, start=True,
                              stop=True).then_inc(s["gm_mm"], 1)
                else:
                    pe.wait_ge(s["gm_done"], g + 1)
                    pe.matmul(misc[:, 288:288 + C], map_d[g][:], step[g][:], start=True, stop=True).then_inc(s["map_mm"], 1)

            def attend(g):
                pe.wait_ge(s["map_done"], g + 1)
                pe.wait_ge(s["z_done"], 2 * g + 1)
                pe.matmul(misc[:, 0:T], map_d[g][:], z[0][g][:], start=True, stop=True).then_inc(s["att_mm"], 1)

            def experts():
                pe.wait_ge(s["ffn_in"], FFN_IN)
                pe.wait_ge(s["z_done"], 2 * G)
                for g in range(G):
                    mm = pe.matmul(misc[g * GB * E:(g + 1) * GB * E, 0:T], gate_w[:], z[1][g][:], start=True, stop=True)
                mm.then_inc(s["lg_mm"], 1)
                pe.wait_ge(s["route_done"], 1)
                for h in range(2):
                    mm = pe.transpose(misc[:, h * P:(h + 1) * P], route[:, h * P:(h + 1) * P], ident)
                mm.then_inc(s["rt_mm"], 1)
                pe.wait_ge(s["rt_done"], 1)
                for g in range(G):
                    for h in range(2):
                        mm = pe.matmul(bank[0][:, g * GB * E:(g + 1) * GB * E], z_t[1][g][:, h, :],
                                       route_t[:, h, g * GB * E:(g + 1) * GB * E], start=(h == 0), stop=(h == 1))
                mm.then_inc(s["pl_mm"], 1)
                pe.wait_ge(s["pl_done"], 1)
                pe.matmul(bank[1][:, 0:P], at["spread"], pool_d[:].rearrange("p g q -> p (g q)"), start=True,
                          stop=True).then_inc(s["sp_mm"], 1)
                pe.matmul(bank[2][:, 0:P], b1[:], at["expert_columns"][0:E, :], start=True, stop=False,
                          skip_group_check=True)
                pe.wait_ge(s["sp_done"], 1)
                for j in range(E // 4):
                    mm = pe.matmul(bank[2][:, 0:P].rearrange("p (i e) -> p i e", e=E)[:, :, 4 * j:4 * j + 4],
                                   w1[:, j, :], pool_e[:, :, 4 * j:4 * j + 4], start=False, stop=(j == E // 4 - 1),
                                   skip_group_check=True)
                mm.then_inc(s["hid_mm"], 1)
                pe.wait_ge(s["hid_done"], 1)
                pe.matmul(bank[3][:], hid[:], w2[:].rearrange("p e o -> p (e o)"), start=True,
                          stop=True).then_inc(s["ex_mm"], 1)
                pe.wait_ge(s["ex_done"], 1)
                for g in range(G):
                    r = slice(g * GB * E, (g + 1) * GB * E)
                    pe.matmul(bank[4 + g][:, 0:T], ex_d[r].rearrange("p b o -> p (b o)"), route[r, :], start=True,
                              stop=True).then_inc(s["y_mm"], 1)

            for g in range(G):
                offsets(g)
                for pr in range(PAIRS):
                    for j in range(BLOCKS):
                        transposes(g, pr, j)
                        if j:
                            sample(g, pr, j - 1)
                    sample(g, pr, BLOCKS - 1)
                    contract(g, pr)
                contract8(g)
            for g in range(G):
                layer_norm(0, g, x1, "x1_done")
                gram_start(g)
                z_back(0, g)
                for l in range(LAYERS):
                    chain_layer(g, l)
                attend(g)
                layer_norm(1, g, x2, "x2_done")
                z_back(1, g)
            experts()


def kernel(x, L0_conv_w_off, L0_conv_b_off, L0_conv_w_dcn, L1_attn_v_matrix, L1_attn_q_matrix,
           L1_ffn_gate_w, L1_ffn_gate_b, L1_ffn_weight1, L1_ffn_weight2):
    import concourse.bacc as bacc
    from concourse.bass_utils import run_bass_kernel_spmd

    f = np.float32
    consts = constants()
    names = list(FIRST) + [n for n in consts if n not in FIRST]
    a = {"table": np.concatenate([consts[n] for n in names], axis=1)}
    a["x"] = np.asarray(x).reshape(G, P, T)

    wo = np.asarray(L0_conv_w_off).reshape(OC, C, TAPS).transpose(1, 2, 0)
    w = np.zeros((GB, C, TAPS, GB, OC), f)
    for b in range(GB):
        w[b, :, :, b] = wo
    a["w_off"] = w.reshape(P, TAPS, GB * OC)
    a["b_off"] = np.zeros((P, 1), f)
    a["b_off"][:GB * OC, 0] = np.tile(np.asarray(L0_conv_b_off), GB)

    wd = np.asarray(L0_conv_w_dcn).reshape(C, C, TAPS).transpose(2, 1, 0)
    a["w_k47"] = np.ascontiguousarray(wd[:8].reshape(2, P, C).transpose(1, 0, 2))
    w8 = np.zeros((GB, C, GB, C), f)
    for b in range(GB):
        w8[b, :, b] = wd[8]
    a["w_k8"] = w8.reshape(P, P)

    q = np.asarray(L1_attn_q_matrix)[:, :, 0].transpose(3, 0, 1, 2).reshape(C, LAYERS, HEADS * C)
    a["q_t"] = np.tile(q, (GB, 1, 1))
    v = np.asarray(L1_attn_v_matrix)[:, :, 0].transpose(3, 0, 1, 2)
    a["v_t"] = np.tile(v, (GB, 1, 1, 1))

    gw = np.zeros((GB, C, GB, E), f)
    for b in range(GB):
        gw[b, :, b] = np.asarray(L1_ffn_gate_w).T
    a["gate_w"] = gw.reshape(P, GB * E)
    a["gate_b"] = np.tile(np.asarray(L1_ffn_gate_b), B).reshape(P, 1)
    w1, w2 = np.asarray(L1_ffn_weight1), np.asarray(L1_ffn_weight2)
    a["w1"] = np.ascontiguousarray(w1[:, :C].reshape(E // 4, P, HID).transpose(1, 0, 2))
    a["b1"] = np.ascontiguousarray(w1[:, C])
    a["w2"] = np.ascontiguousarray(w2[:, :HID].transpose(1, 0, 2))
    a["b2"] = np.tile(w2[:, HID], (B, 1))

    nc = bacc.Bacc("TRN2", target_bir_lowering=False, num_devices=1)
    ap = {n: nc.dram_tensor("in_" + n, v.shape, F32, kind="ExternalInput").ap() for n, v in a.items()}
    ap["out"] = nc.dram_tensor("out", (G, P, T), F32, kind="ExternalOutput").ap()
    build(nc, ap)
    r = run_bass_kernel_spmd(nc, [{"in_" + n: v for n, v in a.items()}], core_ids=[0])
    return r.results[0]["out"].reshape(B, C, H, W)
```

```python
from contextlib import ExitStack

import numpy as np

import concourse.bass as bass
from concourse import mybir

F32 = mybir.dt.float32
ACT = mybir.ActivationFunctionType
ALU = mybir.AluOpType
AX = mybir.AxisListType

B, C, H, W = 8, 32, 16, 16
T = H * W
TAPS, KS = 9, 3
LAYERS, HEADS = 4, 8
E, HID, TOPK = 16, 128, 8
GN_EPS = LN_EPS = 1e-5

P = 128
GB = P // C
G = B // GB
PAIRS = GB // 2
BR = 4
BLOCKS = H // BR
BP = BR * W
UNITS = PAIRS * BLOCKS
WR = P // W
DENSE_ROWS = (0, WR)
LOCAL_ROWS = tuple(min(max(BR * j - 2, 0), H - WR) for j in range(BLOCKS))
NW = len(LOCAL_ROWS)
OC = 2 * TAPS
RING = 3


def constants():
    p = np.arange(P)
    img, ch = p // C, p % C
    t = {}
    t["identity"] = np.eye(P)
    t["same_image"] = (img[:, None] == img[None, :])
    sel = np.zeros((P, GB, OC))
    for b in range(GB):
        sel[b * OC + np.arange(OC), b, np.arange(OC)] = 1
    t["pick_offsets"] = sel
    row_in_block, col = (p % BP) // W, p % W
    k = np.arange(TAPS)
    x = col[:, None] + (k % KS - 1)[None]
    t["dx_base"] = x[:, :, None] - np.arange(W)
    y = row_in_block[:, None, None] + BR * np.arange(BLOCKS)[None, :, None] + (k // KS - 1)[None, None]
    t["dy_local"] = y[..., None] - (np.array(LOCAL_ROWS)[None, :, None, None] + np.arange(WR))
    t["dy_dense"] = y[..., None] - np.arange(H)
    t["layer_identity"] = (ch[:, None] == np.arange(C))
    t["image_expert"] = np.repeat(img[:, None] == np.arange(GB), E, axis=1)
    t["spread"] = (ch[:, None] == ch[None, :])
    t["quarter"] = (img[:, None] == np.arange(GB))
    t["own_expert"] = (p % E)[:, None] == np.arange(E)
    t["own_image"] = (p // E % GB)[:, None] == np.arange(GB)
    t["ones"] = np.ones((P, 1))
    t["expert_columns"] = np.zeros((P, P))
    t["expert_columns"][:E] = np.arange(E)[:, None] == (p % E)[None]
    return {n: np.ascontiguousarray(a.reshape(P, -1).astype(np.float32)) for n, a in t.items()}


FIRST = ("identity", "pick_offsets")


def build(nc, ap):
    consts = constants()
    first_w = sum(consts[n].shape[1] for n in FIRST)
    all_w = sum(a.shape[1] for a in consts.values())
    with ExitStack() as ctx:
        def sb(name, shape):
            return ctx.enter_context(nc.sbuf_tensor(name, shape, F32))

        def sem(name):
            return ctx.enter_context(nc.semaphore(name))

        table = sb("table", [P, all_w])
        at = {}
        o = 0
        for n in list(FIRST) + [n for n in consts if n not in FIRST]:
            at[n] = table[:, o:o + consts[n].shape[1]]
            o += consts[n].shape[1]
        ident = at["identity"]
        same_image3 = at["same_image"].rearrange("p (b c) -> p b c", b=GB)
        x_in = [sb(f"x_in{g}", [P, T]) for g in range(G)]
        w_off = sb("w_off", [P, TAPS, GB * OC])
        b_off = sb("b_off", [P, 1])
        w_k47 = sb("w_k47", [P, 2, C])
        w_k8 = sb("w_k8", [P, P])
        q_t = sb("q_t", [P, LAYERS, HEADS * C])
        v_t = sb("v_t", [P, LAYERS, HEADS, C])
        gate_w = sb("gate_w", [P, GB * E])
        gate_b = sb("gate_b", [P, 1])
        w1 = sb("w1", [P, E // 4, HID])
        b1 = sb("b1", [E, HID])
        w2 = sb("w2", [P, E, C])
        b2 = sb("b2", [P, C])
        gn_stats = sb("gn_stats", [P, G, 6])
        gn_mv = sb("gn_mv", [P, G, 2])
        gn_r = sb("gn_r", [P, G, 5])
        gn_pad = [sb(f"gn_pad{g}", [P, H + 2, W + 2]) for g in range(G)]
        gn = [sb(f"gn{g}", [P, T]) for g in range(G)]
        gn_t = [sb(f"gn_t{g}", [P, NW, P]) for g in range(G)]
        off = [sb(f"off{g}", [GB * OC, T]) for g in range(G)]
        off_t = sb("off_t", [P, G, UNITS * TAPS, 2])
        near = sb("near", [P, G * UNITS * TAPS])
        near_n = sb("near_n", [P, 1])
        is_near = ctx.enter_context(nc.sbuf_tensor("is_near", [1, 1], mybir.dt.int32))
        hat_y = sb("hat_y", [P, G, UNITS * TAPS * H])
        hat_x = sb("hat_x", [P, G, UNITS * TAPS * W])
        hats = sb("hats", [P, 2, TAPS * T])
        wts = sb("wts", [P, 2, BLOCKS * TAPS * 2 * P])
        samp = sb("samp", [P, 2, 2, T])
        samp8 = sb("samp8", [P, T])
        x1 = [sb(f"x1_{g}", [P, T]) for g in range(G)]
        ln_c = [sb(f"ln_c{g}", [P, T]) for g in range(G)]
        ln_sq = [sb(f"ln_sq{g}", [P, T]) for g in range(G)]
        ln_s = [sb(f"ln_s{g}", [P, 2, 7, 2 * GB]) for g in range(G)]
        z_t = [[sb(f"z_t{n}_{g}", [P, 2, P]) for g in range(G)] for n in range(2)]
        z = [[sb(f"z{n}_{g}", [P, T]) for g in range(G)] for n in range(2)]
        gram = [sb(f"gram{g}", [P, P]) for g in range(G)]
        qg = [sb(f"qg{g}", [P, HEADS * C]) for g in range(G)]
        step = [sb(f"step{g}", [P, C]) for g in range(G)]
        step_d = [sb(f"step_d{g}", [P, P]) for g in range(G)]
        ga_m = [sb(f"ga_m{g}", [P, 2, C]) for g in range(G)]
        map_d = [sb(f"map_d{g}", [P, P]) for g in range(G)]
        x2 = [sb(f"x2_{g}", [P, T]) for g in range(G)]
        logit = sb("logit", [P, T])
        logit_r = sb("logit_r", [P, T])
        top = sb("top", [P, TOPK])
        neg_max = sb("neg_max", [P, 1])
        prob = sb("prob", [P, T])
        prob_s = sb("prob_s", [P, 2])
        chosen = sb("chosen", [P, T])
        route = sb("route", [P, T])
        route_t = sb("route_t", [P, 2, P])
        pool_d = sb("pool_d", [P, G, GB * E])
        pool_e = sb("pool_e", [P, G * GB, E])
        hid = sb("hid", [P, P])
        ex_all = sb("ex_all", [P, E, C])
        ex = sb("ex", [P, C])
        ex_b = sb("ex_b", [P, C])
        ex_d = sb("ex_d", [P, GB, C])
        y = [sb(f"y{g}", [P, T]) for g in range(G)]

        bank = [ctx.enter_context(nc.psum_tensor(f"bank{i}", [P, 512], F32)) for i in range(8)]
        ring = bank[:RING]
        smp_ps = [bank[3], bank[4]]
        s8_ps = bank[5]
        conv_ps = bank[6]
        post = [bank[7], bank[6]]
        z_ps = [bank[5], bank[4]]

        s = {n: sem(n) for n in (
            "x0_in", "x1_in", "tab0_in", "tab1_in", "woff_in", "wk_in", "qv_in", "ffn_in",
            "pad_set", "gn_var", "gn_std", "gn_done", "off_mm", "off_done", "gnt_mm", "gnt_done",
            "offt_mm", "offt_done", "dist_x", "abs_x", "hat_x", "dist_y", "abs_y", "hat_y", "near_n", "near_mm", "near_done", "prod", "evac", "smp_mm", "smp_done", "co_mm", "tr_bank",
            "s8_done", "conv_mm", "x1_done",
            "ln_tr", "ln_c", "ln_sq", "ln_var", "ln_std", "zt_done", "z_tr", "z_done",
            "gram_mm", "gram_done", "qg_mm", "qg_done", "st_mm", "st_done", "std_done",
            "ga_mm", "ga_done", "gm_mm", "m_done", "map_mm", "map_done", "att_mm", "x2_done",
            "lg_mm", "lg_done", "top_done", "prob_done", "route_done", "rt_mm", "rt_done",
            "pl_mm", "pl_done", "sp_mm", "sp_done", "hid_mm", "hid_done", "ex_mm", "ex_done",
            "y_mm", "y_done", "out_done", "dve", "act")}

        block = ctx.enter_context(nc.Block())

        def each(stage, *args):
            for g in range(G):
                stage(*args, g)

        def windows(mode, j):
            return (j,) if mode == "local" else (0, NW - 1)

        def banks(mode, n, j):
            nw = len(windows(mode, 0))
            return n * TAPS * nw * BLOCKS // 4 + -(-TAPS * nw * (j + 1) // 4)

        PN = G * PAIRS
        U = PN * BLOCKS

        @block.sync
        def _(sp):
            sp.dma_start(x_in[0][:], ap["x"][0]).then_inc(s["x0_in"], 16)
            sp.dma_start(table[:, :first_w], ap["table"][:, :first_w]).then_inc(s["tab0_in"], 16)
            sp.dma_start(x_in[1][:], ap["x"][1]).then_inc(s["x1_in"], 16)
            sp.dma_start(table[:, first_w:], ap["table"][:, first_w:]).then_inc(s["tab1_in"], 16)
            sp.dma_start(w_k47[:], ap["w_k47"]).then_inc(s["wk_in"], 16)
            sp.dma_start(w_k8[:], ap["w_k8"]).then_inc(s["wk_in"], 16)
            sp.dma_start(q_t[:], ap["q_t"]).then_inc(s["qv_in"], 16)
            sp.dma_start(v_t[:], ap["v_t"]).then_inc(s["qv_in"], 16)
            sp.dma_start(gate_w[:], ap["gate_w"]).then_inc(s["ffn_in"], 16)
            sp.dma_start(gate_b[:], ap["gate_b"]).then_inc(s["ffn_in"], 16)
            sp.dma_start(w1[:], ap["w1"]).then_inc(s["ffn_in"], 16)
            sp.dma_start(b1[:], ap["b1"]).then_inc(s["ffn_in"], 16)
            sp.dma_start(w2[:], ap["w2"]).then_inc(s["ffn_in"], 16)
            sp.dma_start(b2[:], ap["b2"]).then_inc(s["ffn_in"], 16)
            for g in range(G):
                sp.wait_ge(s["y_done"], g + 1)
                sp.dma_start(ap["out"][g], y[g][:]).then_inc(s["out_done"], 16)
            sp.wait_ge(s["out_done"], 16 * G)

        FFN_IN = 16 * 6

        @block.gpsimd
        def _(pool):
            for g in range(G):
                pool.memset(gn_pad[g][:], 0.0).then_inc(s["pad_set"], 1)

        @block.vector
        def _(dve):
            count = [0]

            def link(ins):
                count[0] += 1
                ins.then_inc(s["dve"], 1)
                dve.wait_ge(s["dve"], count[0])

            def newton(r, v, tmp, final, signal):
                link(dve.scalar_tensor_tensor(out=tmp, in0=r, scalar=-0.5, in1=r, op0=ALU.mult, op1=ALU.mult))
                link(dve.tensor_tensor(tmp, tmp, v, ALU.mult))
                ins = dve.scalar_tensor_tensor(out=final, in0=tmp, scalar=1.5, in1=r, op0=ALU.add, op1=ALU.mult)
                link(ins) if signal is None else ins.then_inc(signal, 1)

            def group_norm(g):
                dve.wait_ge(s["x0_in"] if g == 0 else s["x1_in"], 16)
                link(dve.bn_stats(gn_stats[:, g, :], x_in[g][:]))
                link(dve.bn_aggr(gn_mv[:, g, :], gn_stats[:, g, :]))
                r = gn_r
                dve.tensor_scalar(r[:, g, 0:1], gn_mv[:, g, 1:2], GN_EPS, None, ALU.add).then_inc(s["gn_var"], 1)
                dve.wait_ge(s["gn_var"], g + 1)
                dve.wait_ge(s["gn_std"], g + 1)
                link(dve.reciprocal(r[:, g, 2:3], r[:, g, 1:2]))
                newton(r[:, g, 2:3], r[:, g, 0:1], r[:, g, 3:4], r[:, g, 4:5], None)
                dve.wait_ge(s["pad_set"], g + 1)
                dve.tensor_scalar(gn_pad[g][:, 1:H + 1, 1:W + 1], x_in[g][:].rearrange("p (h w) -> p h w", h=H),
                                  gn_mv[:, g, 0:1], r[:, g, 4:5], ALU.subtract, ALU.mult).then_inc(s["gn_done"], 1)
                dve.tensor_scalar(gn[g][:], x_in[g][:], gn_mv[:, g, 0:1], r[:, g, 4:5], ALU.subtract,
                                  ALU.mult).then_inc(s["gn_done"], 1)

            def offsets(g):
                dve.wait_ge(s["offt_mm"], g + 1)
                dve.tensor_copy(off_t[:, g].rearrange("p u a -> p (u a)"),
                                bank[4 + g][:, 0:UNITS * OC]).then_inc(s["offt_done"], 1)
                dve.wait_ge(s["offt_done"], g + 1)

            def columns(g):
                if g == 0:
                    dve.wait_ge(s["tab1_in"], 16)
                dve.tensor_tensor(
                    hat_x[:, g].rearrange("p (u n) -> p u n", u=UNITS).rearrange("p u (k q) -> p u k q", k=TAPS),
                    at["dx_base"].rearrange("p (k q) -> p k q", k=TAPS).unsqueeze(1)
                    .broadcast_to([P, UNITS, TAPS, W]),
                    off_t[:, g, :, 1].rearrange("p (u k) -> p u k", k=TAPS).unsqueeze(3)
                    .broadcast_to([P, UNITS, TAPS, W]),
                    ALU.add).then_inc(s["dist_x"], 1)

            def count_near():
                o = off_t[:].rearrange("p g u a -> p (g u) a")[:, :, 0]
                link(dve.tensor_tensor(near[:], o, o, ALU.mult))
                dve.tensor_scalar(near[:], near[:], 1.0, 0.0, ALU.is_le, ALU.add,
                                  accum_out=near_n[:]).then_inc(s["near_n"], 1)

            def decide():
                dve.wait_ge(s["near_mm"], 1)
                dve.tensor_scalar(is_near[:], bank[0][0:1, 0:1], float(P * G * UNITS * TAPS), None,
                                  ALU.is_ge).then_inc(s["near_done"], 1)

            def rows(mode, g):
                nr = WR if mode == "local" else H
                dve.tensor_tensor(
                    hat_y[:, g, 0:UNITS * TAPS * nr].rearrange("p (r n) -> p r n", r=PAIRS)
                    .rearrange("p r (u q) -> p r u q", q=nr),
                    at["dy_" + mode].rearrange("p (u q) -> p u q", q=nr).unsqueeze(1)
                    .broadcast_to([P, PAIRS, BLOCKS * TAPS, nr]),
                    off_t[:, g, :, 0].rearrange("p (r u) -> p r u", r=PAIRS).unsqueeze(3)
                    .broadcast_to([P, PAIRS, BLOCKS * TAPS, nr]),
                    ALU.add).then_inc(s["dist_y"], 1)

            def product(mode, u):
                nr, g, v = WR if mode == "local" else H, u // UNITS, u % UNITS
                if v == 0:
                    dve.wait_ge(s["hat_x"], g + 1)
                    dve.wait_ge(s["hat_y"], g + 1)
                if u >= 2:
                    dve.wait_ge(s["tr_bank"], banks(mode, (u - 2) // BLOCKS, (u - 2) % BLOCKS))
                hy = hat_y[:, g, v * TAPS * nr:(v + 1) * TAPS * nr].rearrange("p (k q) -> p k q", k=TAPS)
                hx = hat_x[:, g, v * TAPS * W:(v + 1) * TAPS * W].rearrange("p (k q) -> p k q", k=TAPS)
                dve.tensor_tensor(
                    hats[:, u % 2, 0:TAPS * nr * W].rearrange("p (k m) -> p k m", k=TAPS)
                    .rearrange("p k (r q) -> p k r q", q=W),
                    hy.unsqueeze(3).broadcast_to([P, TAPS, nr, W]),
                    hx.unsqueeze(2).broadcast_to([P, TAPS, nr, W]), ALU.mult).then_inc(s["prod"], 1)

            def sampled(n):
                dve.wait_ge(s["smp_mm"], n + 1)
                if n >= 1:
                    dve.wait_ge(s["conv_mm"], 2 * n)
                for i in range(2):
                    dve.tensor_copy(samp[:, i].rearrange("p k t -> p (k t)"), smp_ps[i][:]).then_inc(s["smp_done"], 1)

            def x1_sum(g):
                dve.wait_ge(s["co_mm"], g + 1)
                dve.tensor_tensor(x1[g][:], conv_ps[:, 0:T], x_in[g][:], ALU.add).then_inc(s["x1_done"], 1)

            def convolve(mode):
                rows(mode, 0)
                rows(mode, 1)
                for u in range(U):
                    product(mode, u)
                    n, j = divmod(u, BLOCKS)
                    if j == 1 and n >= 1:
                        sampled(n - 1)
                    if j == 2 and n >= 1 and n % PAIRS == 0:
                        x1_sum(n // PAIRS - 1)
                sampled(PN - 1)
                x1_sum(G - 1)

            seg = lambda a: a.rearrange("p (s c) -> p s c", c=C)

            def layer_norm(n):
                each(ln_center, n)
                each(ln_variance, n)
                each(ln_scale, n)

            def ln_center(n, g):
                i, st = n * G + g, ln_s[g][:, n]
                dve.wait_ge(s["ln_tr"], i + 1)
                link(dve.tensor_reduce(st[:, 0, :], seg(post[g][:, 0:T]), AX.X, ALU.add))
                dve.scalar_tensor_tensor(out=seg(ln_c[g][:]), in0=st[:, 0, :].unsqueeze(2).broadcast_to([P, 2 * GB, C]),
                                         scalar=-1.0 / C, in1=seg(post[g][:, 0:T]), op0=ALU.mult,
                                         op1=ALU.add).then_inc(s["ln_c"], 1)

            def ln_variance(n, g):
                i, st = n * G + g, ln_s[g][:, n]
                dve.wait_ge(s["ln_sq"], i + 1)
                link(dve.tensor_reduce(st[:, 1, :], seg(ln_sq[g][:]), AX.X, ALU.add))
                dve.tensor_scalar(st[:, 2, :], st[:, 1, :], 1.0 / C, LN_EPS, ALU.mult, ALU.add).then_inc(s["ln_var"], 1)

            def ln_scale(n, g):
                i, st = n * G + g, ln_s[g][:, n]
                dve.wait_ge(s["ln_var"], i + 1)
                dve.wait_ge(s["ln_std"], i + 1)
                link(dve.reciprocal(st[:, 4, :], st[:, 3, :]))
                newton(st[:, 4, :], st[:, 2, :], st[:, 5, :], st[:, 6, :], None)
                dve.wait_ge(s["ln_c"], i + 1)
                dve.tensor_tensor(seg(z_t[n][g][:].rearrange("p h q -> p (h q)")), seg(ln_c[g][:]),
                                  st[:, 6, :].unsqueeze(2).broadcast_to([P, 2 * GB, C]),
                                  ALU.mult).then_inc(s["zt_done"], 1)

            def spread_diag(out, compact, signal):
                dve.tensor_tensor(out.rearrange("p (b c) -> p b c", b=GB),
                                  compact.unsqueeze(1).broadcast_to([P, GB, C]), same_image3,
                                  ALU.mult).then_inc(signal, 1)

            def gram_start(g):
                dve.wait_ge(s["gram_mm"], g + 1)
                dve.tensor_tensor(gram[g][:], post[g][:, 0:P], at["same_image"], ALU.mult).then_inc(s["gram_done"], 1)

            def chain_step(l, g):
                n = l * G + g
                dve.wait_ge(s["gram_done"], n + 1)
                dve.wait_ge(s["st_mm"], n + 1)
                dve.scalar_tensor_tensor(out=step[g][:], in0=post[g][:, 256:256 + C], scalar=1.0 / (T * HEADS),
                                         in1=at["layer_identity"], op0=ALU.mult, op1=ALU.add).then_inc(s["st_done"], 1)
                dve.wait_ge(s["st_done"], n + 1)
                if l < LAYERS - 1:
                    spread_diag(step_d[g][:], step[g][:], s["std_done"])

            def chain_gram(l, g):
                n = l * G + g
                if l < LAYERS - 1:
                    dve.wait_ge(s["ga_mm"], n + 1)
                    dve.tensor_copy(ga_m[g][:, 0], post[g][:, 288:288 + C]).then_inc(s["ga_done"], 1)
                else:
                    dve.wait_ge(s["map_mm"], g + 1)
                    spread_diag(map_d[g][:], post[g][:, 288:288 + C], s["map_done"])

            def chain_next(l, g):
                n = l * G + g
                dve.wait_ge(s["gm_mm"], n + 1)
                if l < LAYERS - 2:
                    dve.tensor_copy(ga_m[g][:, 1], post[g][:, 320 + C:320 + 2 * C]).then_inc(s["m_done"], 1)
                else:
                    spread_diag(map_d[g][:], post[g][:, 320 + C:320 + 2 * C], s["m_done"])
                spread_diag(gram[g][:], post[g][:, 320:320 + C], s["gram_done"])

            def x2_sum(g):
                dve.wait_ge(s["att_mm"], g + 1)
                dve.tensor_tensor(x2[g][:], post[g][:, 0:T], x1[g][:], ALU.add).then_inc(s["x2_done"], 1)

            def experts():
                dve.wait_ge(s["lg_done"], 1)
                dve.max(top[:], logit[:]).then_inc(s["top_done"], 1)
                dve.wait_ge(s["top_done"], 1)
                dve.tensor_scalar(neg_max[:], top[:, 0:1], -1.0, None, ALU.mult).then_inc(s["top_done"], 1)
                link(dve.match_replace(logit_r[:], top[:], logit[:], -3.0e38))
                link(dve.tensor_tensor(chosen[:], logit[:], logit_r[:], ALU.not_equal))
                dve.wait_ge(s["prob_done"], 1)
                link(dve.reciprocal(prob_s[:, 1:2], prob_s[:, 0:1]))
                dve.scalar_tensor_tensor(out=route[:], in0=prob[:], scalar=prob_s[:, 1:2], in1=chosen[:],
                                         op0=ALU.mult, op1=ALU.mult).then_inc(s["route_done"], 1)
                dve.wait_ge(s["rt_mm"], 1)
                dve.tensor_copy(route_t[:].rearrange("p h q -> p (h q)"), bank[7][:, 0:2 * P]).then_inc(s["rt_done"], 1)
                dve.wait_ge(s["pl_mm"], 1)
                dve.tensor_tensor(pool_d[:], bank[0][:, 0:P].rearrange("p (g q) -> p g q", g=G),
                                  at["image_expert"].unsqueeze(1).broadcast_to([P, G, GB * E]),
                                  ALU.mult).then_inc(s["pl_done"], 1)
                dve.wait_ge(s["sp_mm"], 1)
                dve.tensor_tensor(pool_e[:].rearrange("p i (j r) -> p (i j) r", r=4),
                                  bank[1][:, 0:P].rearrange("p (n r) -> p n r", r=4),
                                  at["quarter"].unsqueeze(1).broadcast_to([P, P // 4, 4]),
                                  ALU.mult).then_inc(s["sp_done"], 1)
                dve.wait_ge(s["ex_mm"], 1)
                link(dve.tensor_tensor(ex_all[:], bank[3][:].rearrange("p (e o) -> p e o", e=E),
                                       at["own_expert"].unsqueeze(2).broadcast_to([P, E, C]), ALU.mult))
                link(dve.tensor_reduce(ex[:], ex_all[:].rearrange("p e o -> p o e"), AX.X, ALU.add))
                link(dve.tensor_tensor(ex_b[:], ex[:], b2[:], ALU.add))
                dve.tensor_tensor(ex_d[:], ex_b[:].unsqueeze(1).broadcast_to([P, GB, C]),
                                  at["own_image"].unsqueeze(2).broadcast_to([P, GB, C]),
                                  ALU.mult).then_inc(s["ex_done"], 1)
                for g in range(G):
                    dve.wait_ge(s["y_mm"], g + 1)
                    dve.tensor_tensor(y[g][:], bank[4 + g][:, 0:T], x2[g][:], ALU.add).then_inc(s["y_done"], 1)

            for g in range(G):
                group_norm(g)
            for g in range(G):
                offsets(g)
                columns(g)
            count_near()
            decide()
            dve.wait_ge(s["near_done"], 1)
            near_flag = dve.value_load(is_near[0:1, 0:1], min_val=0, max_val=1)
            with dve.If(near_flag):
                convolve("local")
            with dve.Else():
                convolve("dense")
            layer_norm(0)
            each(gram_start)
            for l in range(LAYERS):
                each(chain_step, l)
                each(chain_gram, l)
                if l < LAYERS - 1:
                    each(chain_next, l)
            each(x2_sum)
            layer_norm(1)
            dve.wait_ge(s["ffn_in"], FFN_IN)
            experts()

        @block.scalar
        def _(act):
            act.dma_start(w_off[:], ap["w_off"]).then_inc(s["woff_in"], 16)
            act.dma_start(b_off[:], ap["b_off"]).then_inc(s["woff_in"], 16)

            def group_norm(g):
                act.wait_ge(s["gn_var"], g + 1)
                act.activation(gn_r[:, g, 1:2], gn_r[:, g, 0:1], ACT.Sqrt).then_inc(s["gn_std"], 1)

            def offsets(g):
                act.wait_ge(s["off_mm"], g + 1)
                if g == 0:
                    act.wait_ge(s["woff_in"], 32)
                act.activation(off[g][:], bank[g][0:GB * OC, 0:T], ACT.Identity,
                               bias=b_off[0:GB * OC, 0:1]).then_inc(s["off_done"], 1)
                act.wait_ge(s["gnt_mm"], g + 1)
                act.copy(gn_t[g][:].rearrange("p w q -> p (w q)"), bank[2 + g][:]).then_inc(s["gnt_done"], 1)

            def hat(buf, size, g, dist, absd, done):
                d = buf[:, g, 0:size]
                act.wait_ge(s[dist], g + 1)
                act.activation(d, d, ACT.Abs).then_inc(s[absd], 1)
                act.wait_ge(s[absd], g + 1)
                act.activation(d, d, ACT.Relu, bias=1.0, scale=-1.0).then_inc(s[done], 1)

            def samp8_copy(g):
                act.wait_ge(s["smp_mm"], (g + 1) * PAIRS)
                if g >= 1:
                    act.wait_ge(s["co_mm"], g)
                act.copy(samp8[:], s8_ps[:, 0:T]).then_inc(s["s8_done"], 1)

            def convolve(mode):
                nr, nw = (WR, 1) if mode == "local" else (H, 2)
                for g in range(G):
                    hat(hat_y, UNITS * TAPS * nr, g, "dist_y", "abs_y", "hat_y")
                per = TAPS * BLOCKS * nw // 4
                for n in range(PN):
                    if n >= 2:
                        act.wait_ge(s["smp_mm"], n - 1)
                    for i in range(per):
                        if n >= 1 and n % PAIRS == 0 and i == TAPS * nw // 4:
                            samp8_copy(n // PAIRS - 1)
                        f = n * per + i
                        act.wait_ge(s["tr_bank"], f + 1)
                        act.copy(wts[:, n % 2, 512 * i:512 * i + 512], ring[f % RING][:]).then_inc(s["evac"], 1)
                samp8_copy(G - 1)

            def ln_square(n, g):
                act.wait_ge(s["ln_c"], n * G + g + 1)
                act.activation(ln_sq[g][:], ln_c[g][:], ACT.Square).then_inc(s["ln_sq"], 1)

            def ln_root(n, g):
                act.wait_ge(s["ln_var"], n * G + g + 1)
                act.activation(ln_s[g][:, n, 3, :], ln_s[g][:, n, 2, :], ACT.Sqrt).then_inc(s["ln_std"], 1)

            def z_copy(n, g):
                act.wait_ge(s["z_tr"], n * G + g + 1)
                act.copy(z[n][g][:], z_ps[g][:, 0:T]).then_inc(s["z_done"], 1)

            def qg_copy(l, g):
                act.wait_ge(s["qg_mm"], l * G + g + 1)
                act.copy(qg[g][:], post[g][:, 0:HEADS * C]).then_inc(s["qg_done"], 1)

            for g in range(G):
                group_norm(g)
            for g in range(G):
                offsets(g)
                hat(hat_x, UNITS * TAPS * W, g, "dist_x", "abs_x", "hat_x")
            act.wait_ge(s["near_done"], 1)
            near_flag = act.value_load(is_near[0:1, 0:1], min_val=0, max_val=1)
            with act.If(near_flag):
                convolve("local")
            with act.Else():
                convolve("dense")
            each(ln_square, 0)
            each(ln_root, 0)
            each(z_copy, 0)
            for l in range(LAYERS):
                each(qg_copy, l)
            each(ln_square, 1)
            each(ln_root, 1)
            each(z_copy, 1)
            act.wait_ge(s["ffn_in"], FFN_IN)
            act.wait_ge(s["lg_mm"], 1)
            act.activation(logit[:], bank[7][:, 0:T], ACT.Identity, bias=gate_b[:, 0:1]).then_inc(s["lg_done"], 1)
            act.wait_ge(s["lg_done"], 1)
            act.wait_ge(s["top_done"], 2)
            act.activation(prob[:], logit[:], ACT.Exp, bias=neg_max[:, 0:1],
                           accum_out=prob_s[:, 0:1]).then_inc(s["prob_done"], 1)
            act.wait_ge(s["hid_mm"], 1)
            act.activation(hid[:], bank[2][:, 0:P], ACT.Gelu).then_inc(s["hid_done"], 1)

        @block.tensor
        def _(pe):
            def offsets(g):
                pe.wait_ge(s["gn_done"], 2 * g + 1)
                if g == 0:
                    pe.wait_ge(s["woff_in"], 32)
                for t in range(TAPS):
                    dy, dx = divmod(t, KS)
                    mm = pe.matmul(bank[g][0:GB * OC, 0:T], w_off[:, t, :], gn_pad[g][:, dy:dy + H, dx:dx + W],
                                   start=(t == 0), stop=(t == TAPS - 1))
                mm.then_inc(s["off_mm"], 1)

            def windows_t(g):
                pe.wait_ge(s["gn_done"], 2 * g + 2)
                if g == 0:
                    pe.wait_ge(s["tab0_in"], 16)
                for w, r in enumerate(LOCAL_ROWS):
                    mm = pe.transpose(bank[2 + g][:, w * P:(w + 1) * P], gn[g][:, r * W:(r + WR) * W], ident)
                mm.then_inc(s["gnt_mm"], 1)

            def offsets_t(g):
                pe.wait_ge(s["off_done"], g + 1)
                for v in range(UNITS):
                    pr, j = divmod(v, BLOCKS)
                    for i in range(2):
                        mm = pe.matmul(bank[4 + g][i * BP:(i + 1) * BP, v * OC:(v + 1) * OC],
                                       off[g][:, j * BP:(j + 1) * BP],
                                       at["pick_offsets"][0:GB * OC, (2 * pr + i) * OC:(2 * pr + i + 1) * OC],
                                       start=True, stop=True)
                mm.then_inc(s["offt_mm"], 1)

            def count_near():
                pe.wait_ge(s["tab1_in"], 16)
                pe.wait_ge(s["off_done"], G)
                pe.wait_ge(s["near_n"], 1)
                pe.matmul(bank[0][0:1, 0:1], near_n[:], at["ones"], start=True, stop=True).then_inc(s["near_mm"], 1)

            def transposes(mode, u):
                n, j = divmod(u, BLOCKS)
                nw = len(windows(mode, 0))
                per = TAPS * BLOCKS * nw // 4
                pe.wait_ge(s["prod"], u + 1)
                for i in range(TAPS * nw):
                    slot = j * TAPS * nw + i
                    f = n * per + slot // 4
                    if slot % 4 == 0 and f >= RING:
                        pe.wait_ge(s["evac"], f - RING + 1)
                    mm = pe.transpose(ring[f % RING][:, (slot % 4) * P:(slot % 4 + 1) * P],
                                      hats[:, u % 2, i * P:(i + 1) * P], ident)
                    if slot % 4 == 3:
                        mm.then_inc(s["tr_bank"], 1)

            def sample(mode, u):
                n, j = divmod(u, BLOCKS)
                g, pr = divmod(n, PAIRS)
                nw = len(windows(mode, 0))
                if j == 0 and n:
                    pe.wait_ge(s["smp_done"], 2 * n)
                if j == 0 and pr == 0:
                    pe.wait_ge(s["gnt_done"], g + 1)
                    if g:
                        pe.wait_ge(s["s8_done"], g)
                pe.wait_ge(s["evac"], banks(mode, n, j))
                w = wts[:, n % 2, 0:BLOCKS * TAPS * nw * P].rearrange("q (j k m) -> q j k m", j=BLOCKS, k=TAPS)
                w = w.rearrange("q j k (h i p) -> q j k h i p", h=nw, i=2)
                for i in range(2):
                    b = 2 * pr + i
                    for h, win in enumerate(windows(mode, j)):
                        lhs = gn_t[g][:, win, b * C:(b + 1) * C]
                        for jj in range(4):
                            pe.matmul(
                                smp_ps[i][jj * C:(jj + 1) * C, :].rearrange("p (k t) -> p k t", k=2)[:, :, j * BP:(j + 1) * BP],
                                lhs, w[:, j, jj:TAPS - 1:4, h, i, :], start=(h == 0), stop=(h == nw - 1),
                                tile_position=(0, jj * C))
                        mm = pe.matmul(s8_ps[b * C:(b + 1) * C, j * BP:(j + 1) * BP], lhs, w[:, j, TAPS - 1, h, i, :],
                                       start=(h == 0), stop=(h == nw - 1), tile_position=(0, b * C))
                if j == BLOCKS - 1:
                    mm.then_inc(s["smp_mm"], 1)

            def contract(n):
                g, pr = divmod(n, PAIRS)
                if n == 0:
                    pe.wait_ge(s["wk_in"], 32)
                if pr == 0 and g:
                    pe.wait_ge(s["x1_done"], g)
                pe.wait_ge(s["smp_done"], 2 * (n + 1))
                for i in range(2):
                    b = 2 * pr + i
                    for k in range(2):
                        mm = pe.matmul(conv_ps[b * C:(b + 1) * C, 0:T], w_k47[:, k, :], samp[:, i, k, :],
                                       start=(k == 0), stop=False, tile_position=(0, b * C), skip_group_check=True)
                    mm.then_inc(s["conv_mm"], 1)
                if pr == PAIRS - 1:
                    pe.wait_ge(s["s8_done"], g + 1)
                    pe.matmul(conv_ps[:, 0:T], w_k8[:], samp8[:], start=False, stop=True,
                              skip_group_check=True).then_inc(s["co_mm"], 1)

            def convolve(mode):
                for u in range(U):
                    transposes(mode, u)
                    if u >= BLOCKS and u % BLOCKS == 1:
                        contract(u // BLOCKS - 1)
                    if u:
                        sample(mode, u - 1)
                sample(mode, U - 1)
                contract(PN - 1)

            def ln_tokens(n, g):
                src, done = ((x1, "x1_done"), (x2, "x2_done"))[n]
                pe.wait_ge(s[done], g + 1)
                for h in range(2):
                    mm = pe.transpose(post[g][:, h * P:(h + 1) * P], src[g][:, h * P:(h + 1) * P], ident)
                mm.then_inc(s["ln_tr"], 1)

            def z_back(n, g):
                pe.wait_ge(s["zt_done"], n * G + g + 1)
                for h in range(2):
                    mm = pe.transpose(z_ps[g][:, h * P:(h + 1) * P], z_t[n][g][:, h, :], ident)
                mm.then_inc(s["z_tr"], 1)

            def gram_start(g):
                pe.wait_ge(s["zt_done"], g + 1)
                for h in range(2):
                    mm = pe.matmul(post[g][:, 0:P], z_t[0][g][:, h, :], z_t[0][g][:, h, :], start=(h == 0), stop=(h == 1))
                mm.then_inc(s["gram_mm"], 1)

            def chain_heads(l, g):
                if l:
                    pe.wait_ge(s["m_done"], (l - 1) * G + g + 1)
                pe.wait_ge(s["gram_done"], l * G + g + 1)
                pe.matmul(post[g][:, 0:HEADS * C], gram[g][:], q_t[:, l, :], start=True, stop=True).then_inc(s["qg_mm"], 1)

            def chain_step(l, g):
                pe.wait_ge(s["qg_done"], l * G + g + 1)
                for h in range(HEADS):
                    for b in range(GB):
                        r = slice(b * C, (b + 1) * C)
                        mm = pe.matmul(post[g][r, 256:256 + C], qg[g][r, h * C:(h + 1) * C], v_t[r, l, h, :],
                                       start=(h == 0), stop=(h == HEADS - 1), tile_position=(b * C, b * C),
                                       skip_group_check=True)
                mm.then_inc(s["st_mm"], 1)

            def chain_gram(l, g):
                n = l * G + g
                pe.wait_ge(s["st_done"], n + 1)
                if l < LAYERS - 1:
                    pe.matmul(post[g][:, 288:288 + C], gram[g][:], step[g][:], start=True,
                              stop=True).then_inc(s["ga_mm"], 1)
                else:
                    pe.wait_ge(s["m_done"], n - G + 1)
                    pe.matmul(post[g][:, 288:288 + C], map_d[g][:], step[g][:], start=True,
                              stop=True).then_inc(s["map_mm"], 1)

            def chain_next(l, g):
                n = l * G + g
                if l:
                    pe.wait_ge(s["m_done"], n - G + 1)
                pe.wait_ge(s["std_done"], n + 1)
                pe.wait_ge(s["ga_done"], n + 1)
                mt = at["layer_identity"] if l == 0 else ga_m[g][:, 1]
                pe.matmul(post[g][:, 320 + C:320 + 2 * C], step_d[g][:], mt, start=True, stop=True)
                pe.matmul(post[g][:, 320:320 + C], step_d[g][:], ga_m[g][:, 0], start=True,
                          stop=True).then_inc(s["gm_mm"], 1)

            def attend(g):
                pe.wait_ge(s["map_done"], g + 1)
                pe.wait_ge(s["z_done"], g + 1)
                pe.matmul(post[g][:, 0:T], map_d[g][:], z[0][g][:], start=True, stop=True).then_inc(s["att_mm"], 1)

            def experts():
                pe.wait_ge(s["ffn_in"], FFN_IN)
                pe.wait_ge(s["z_done"], 2 * G)
                for g in range(G):
                    mm = pe.matmul(bank[7][g * GB * E:(g + 1) * GB * E, 0:T], gate_w[:], z[1][g][:], start=True, stop=True)
                mm.then_inc(s["lg_mm"], 1)
                pe.wait_ge(s["route_done"], 1)
                for h in range(2):
                    mm = pe.transpose(bank[7][:, h * P:(h + 1) * P], route[:, h * P:(h + 1) * P], ident)
                mm.then_inc(s["rt_mm"], 1)
                pe.wait_ge(s["rt_done"], 1)
                for g in range(G):
                    for h in range(2):
                        mm = pe.matmul(bank[0][:, g * GB * E:(g + 1) * GB * E], z_t[1][g][:, h, :],
                                       route_t[:, h, g * GB * E:(g + 1) * GB * E], start=(h == 0), stop=(h == 1))
                mm.then_inc(s["pl_mm"], 1)
                pe.wait_ge(s["pl_done"], 1)
                pe.matmul(bank[1][:, 0:P], at["spread"], pool_d[:].rearrange("p g q -> p (g q)"), start=True,
                          stop=True).then_inc(s["sp_mm"], 1)
                pe.matmul(bank[2][:, 0:P], b1[:], at["expert_columns"][0:E, :], start=True, stop=False,
                          skip_group_check=True)
                pe.wait_ge(s["sp_done"], 1)
                for j in range(E // 4):
                    mm = pe.matmul(bank[2][:, 0:P].rearrange("p (i e) -> p i e", e=E)[:, :, 4 * j:4 * j + 4],
                                   w1[:, j, :], pool_e[:, :, 4 * j:4 * j + 4], start=False, stop=(j == E // 4 - 1),
                                   skip_group_check=True)
                mm.then_inc(s["hid_mm"], 1)
                pe.wait_ge(s["hid_done"], 1)
                pe.matmul(bank[3][:], hid[:], w2[:].rearrange("p e o -> p (e o)"), start=True,
                          stop=True).then_inc(s["ex_mm"], 1)
                pe.wait_ge(s["ex_done"], 1)
                for g in range(G):
                    r = slice(g * GB * E, (g + 1) * GB * E)
                    pe.matmul(bank[4 + g][:, 0:T], ex_d[r].rearrange("p b o -> p (b o)"), route[r, :], start=True,
                              stop=True).then_inc(s["y_mm"], 1)

            for g in range(G):
                offsets(g)
                windows_t(g)
            for g in range(G):
                offsets_t(g)
            count_near()
            pe.wait_ge(s["near_done"], 1)
            near_flag = pe.value_load(is_near[0:1, 0:1], min_val=0, max_val=1)
            with pe.If(near_flag):
                convolve("local")
            with pe.Else():
                convolve("dense")
            pe.wait_ge(s["qv_in"], 32)
            each(ln_tokens, 0)
            each(gram_start)
            each(z_back, 0)
            for l in range(LAYERS):
                each(chain_heads, l)
                each(chain_step, l)
                each(chain_gram, l)
                if l < LAYERS - 1:
                    each(chain_next, l)
            each(attend)
            each(ln_tokens, 1)
            each(z_back, 1)
            experts()


def kernel(x, L0_conv_w_off, L0_conv_b_off, L0_conv_w_dcn, L1_attn_v_matrix, L1_attn_q_matrix,
           L1_ffn_gate_w, L1_ffn_gate_b, L1_ffn_weight1, L1_ffn_weight2):
    import concourse.bacc as bacc
    from concourse.bass_utils import run_bass_kernel_spmd

    f = np.float32
    consts = constants()
    names = list(FIRST) + [n for n in consts if n not in FIRST]
    a = {"table": np.concatenate([consts[n] for n in names], axis=1)}
    a["x"] = np.asarray(x).reshape(G, P, T)

    wo = np.asarray(L0_conv_w_off).reshape(OC, C, TAPS).transpose(1, 2, 0)
    w = np.zeros((GB, C, TAPS, GB, OC), f)
    for b in range(GB):
        w[b, :, :, b] = wo
    a["w_off"] = w.reshape(P, TAPS, GB * OC)
    a["b_off"] = np.zeros((P, 1), f)
    a["b_off"][:GB * OC, 0] = np.tile(np.asarray(L0_conv_b_off), GB)

    wd = np.asarray(L0_conv_w_dcn).reshape(C, C, TAPS).transpose(2, 1, 0)
    a["w_k47"] = np.ascontiguousarray(wd[:8].reshape(2, P, C).transpose(1, 0, 2))
    w8 = np.zeros((GB, C, GB, C), f)
    for b in range(GB):
        w8[b, :, b] = wd[8]
    a["w_k8"] = w8.reshape(P, P)

    q = np.asarray(L1_attn_q_matrix)[:, :, 0].transpose(3, 0, 1, 2).reshape(C, LAYERS, HEADS * C)
    a["q_t"] = np.tile(q, (GB, 1, 1))
    v = np.asarray(L1_attn_v_matrix)[:, :, 0].transpose(3, 0, 1, 2)
    a["v_t"] = np.tile(v, (GB, 1, 1, 1))

    gw = np.zeros((GB, C, GB, E), f)
    for b in range(GB):
        gw[b, :, b] = np.asarray(L1_ffn_gate_w).T
    a["gate_w"] = gw.reshape(P, GB * E)
    a["gate_b"] = np.tile(np.asarray(L1_ffn_gate_b), B).reshape(P, 1)
    w1, w2 = np.asarray(L1_ffn_weight1), np.asarray(L1_ffn_weight2)
    a["w1"] = np.ascontiguousarray(w1[:, :C].reshape(E // 4, P, HID).transpose(1, 0, 2))
    a["b1"] = np.ascontiguousarray(w1[:, C])
    a["w2"] = np.ascontiguousarray(w2[:, :HID].transpose(1, 0, 2))
    a["b2"] = np.tile(w2[:, HID], (B, 1))

    nc = bacc.Bacc("TRN2", target_bir_lowering=False, num_devices=1)
    ap = {n: nc.dram_tensor("in_" + n, v.shape, F32, kind="ExternalInput").ap() for n, v in a.items()}
    ap["out"] = nc.dram_tensor("out", (G, P, T), F32, kind="ExternalOutput").ap()
    build(nc, ap)
    r = run_bass_kernel_spmd(nc, [{"in_" + n: v for n, v in a.items()}], core_ids=[0])
    return r.results[0]["out"].reshape(B, C, H, W)
```

```python
from contextlib import ExitStack

import numpy as np

import concourse.bass as bass
from concourse import mybir

F32 = mybir.dt.float32
ACT = mybir.ActivationFunctionType
ALU = mybir.AluOpType
AX = mybir.AxisListType

B, C, H, W = 8, 32, 16, 16
T = H * W
TAPS, KS = 9, 3
LAYERS, HEADS = 4, 8
E, HID, TOPK = 16, 128, 8
EPS = 1e-5

P = 128
GB = P // C
G = B // GB
PAIRS = GB // 2
BR = 4
BLOCKS = H // BR
BP = BR * W
UNITS = PAIRS * BLOCKS
WR = P // W
DENSE_ROWS = (0, WR)
LOCAL_ROWS = tuple(min(max(BR * j - 2, 0), H - WR) for j in range(BLOCKS))
NW = len(LOCAL_ROWS)
OC = 2 * TAPS
HATS = {"local": 4, "dense": 2}
RING = 3


def constants():
    p = np.arange(P)
    img, ch = p // C, p % C
    t = {}
    t["identity"] = np.eye(P)
    t["same_image"] = (img[:, None] == img[None, :])
    sel = np.zeros((P, GB, OC))
    for b in range(GB):
        sel[b * OC + np.arange(OC), b, np.arange(OC)] = 1
    t["pick_offsets"] = sel
    row_in_block, col = (p % BP) // W, p % W
    k = np.arange(TAPS)
    x = col[:, None] + (k % KS - 1)[None]
    t["dx_base"] = x[:, :, None] - np.arange(W)
    y = row_in_block[:, None, None] + BR * np.arange(BLOCKS)[None, :, None] + (k // KS - 1)[None, None]
    t["dy_base"] = y[..., None] - np.arange(H)
    t["row_channels"] = ((p < GB * OC) & (p % 2 == 0))
    t["first_identity"] = (p[:, None] == ch[None, :])
    t["center"] = (img[:, None] == img[None, :]) * ((ch[:, None] == ch[None, :]) - 1.0 / C)
    t["spread"] = (ch[:, None] == ch[None, :])
    t["image_expert"] = np.tile(img[:, None] == np.arange(GB), (1, E))
    t["quarter_expert"] = (img[:, None] == np.arange(E) % GB)
    t["own_image"] = (p % B)[:, None] == np.arange(B)
    t["expert_columns"] = np.zeros((P, P))
    t["expert_columns"][:E] = np.arange(E)[:, None] == (p // B)[None]
    return {n: np.ascontiguousarray(a.reshape(P, -1).astype(np.float32)) for n, a in t.items()}


FIRST = ("identity", "pick_offsets")


def build(nc, ap):
    consts = constants()
    first_w = sum(consts[n].shape[1] for n in FIRST)
    all_w = sum(a.shape[1] for a in consts.values())
    with ExitStack() as ctx:
        def sb(name, shape):
            return ctx.enter_context(nc.sbuf_tensor(name, shape, F32))

        def sem(name):
            return ctx.enter_context(nc.semaphore(name))

        table = sb("table", [P, all_w])
        at = {}
        o = 0
        for n in list(FIRST) + [n for n in consts if n not in FIRST]:
            at[n] = table[:, o:o + consts[n].shape[1]]
            o += consts[n].shape[1]
        ident = at["identity"]
        same_image3 = at["same_image"].rearrange("p (b c) -> p b c", b=GB)
        x_in = [sb(f"x_in{g}", [P, T]) for g in range(G)]
        w_off = sb("w_off", [P, TAPS, GB * OC])
        b_off = sb("b_off", [P, 1])
        w_k47 = sb("w_k47", [P, 2, C])
        w_k8 = sb("w_k8", [P, P])
        q_t = sb("q_t", [P, LAYERS, HEADS * C])
        v_t = sb("v_t", [P, LAYERS, HEADS, C])
        v_d = sb("v_d", [P, LAYERS, HEADS, P])
        gate_w = sb("gate_w", [P, G, P])
        gate_b = sb("gate_b", [E, T])
        w1 = sb("w1", [P, E // 4, HID])
        b1 = sb("b1", [E, HID])
        w2 = sb("w2", [P, E, C])
        b2 = sb("b2", [E, C])
        warm = sb("warm", [P, T])
        eps = sb("eps", [P, 1])
        gn_stats = sb("gn_stats", [P, G, 6])
        gn_mv = sb("gn_mv", [P, G, 2])
        gn_r = sb("gn_r", [P, G, 6])
        gn_pad = [sb(f"gn_pad{g}", [P, H + 2, W + 2]) for g in range(G)]
        gn = [sb(f"gn{g}", [P, T]) for g in range(G)]
        gn_t = [sb(f"gn_t{g}", [P, NW, P]) for g in range(G)]
        off = [sb(f"off{g}", [GB * OC, T]) for g in range(G)]
        off_t = sb("off_t", [P, G, UNITS * TAPS, 2])
        near_max = sb("near_max", [GB * OC, G])
        near_n = sb("near_n", [GB * OC, 1])
        is_near = ctx.enter_context(nc.sbuf_tensor("is_near", [1, 1], mybir.dt.int32))
        hat_y = sb("hat_y", [P, G, UNITS * TAPS * H])
        hat_x = sb("hat_x", [P, G, UNITS * TAPS * W])
        hats = sb("hats", [P, 2 * TAPS * T])
        wts = sb("wts", [P, 2, BLOCKS * TAPS * 2 * P])
        samp = sb("samp", [P, 2, 2, T])
        samp8 = sb("samp8", [P, T])
        x1 = [sb(f"x1_{g}", [P, T]) for g in range(G)]
        ln_sq = [sb(f"ln_sq{g}", [P, T]) for g in range(G)]
        ln_s = sb("ln_s", [P, 2, 7, G, 2 * GB])
        z_t = [[sb(f"z_t{n}_{g}", [P, 2, P]) for g in range(G)] for n in range(2)]
        z = [[sb(f"z{n}_{g}", [P, T]) for g in range(G)] for n in range(2)]
        gram = [sb(f"gram{g}", [P, P]) for g in range(G)]
        qg = [sb(f"qg{g}", [P, HEADS * C]) for g in range(G)]
        part = [sb(f"part{g}", [P, P]) for g in range(G)]
        step = [sb(f"step{g}", [P, P]) for g in range(G)]
        ga = [sb(f"ga{g}", [P, P]) for g in range(G)]
        gram_r = [sb(f"gram_r{g}", [P, P]) for g in range(G)]
        x2 = [sb(f"x2_{g}", [P, T]) for g in range(G)]
        logit_r = sb("logit_r", [P, T])
        top = sb("top", [P, TOPK])
        neg_max = sb("neg_max", [P, 1])
        prob = sb("prob", [P, T])
        prob_s = sb("prob_s", [P, 2])
        chosen = sb("chosen", [P, T])
        route = sb("route", [P, T])
        route_t = sb("route_t", [P, 2, P])
        pool_d = sb("pool_d", [P, G, GB * E])
        pool_e = sb("pool_e", [P, E, B])
        hid_d = sb("hid_d", [P, 4, 4 * 5 * B])
        ex_d = sb("ex_d", [P, B, C])
        y = [sb(f"y{g}", [P, T]) for g in range(G)]

        bank = [ctx.enter_context(nc.psum_tensor(f"bank{i}", [P, 512], F32)) for i in range(8)]
        ring = bank[:RING]
        smp_ps = [bank[3], bank[4]]
        s8_ps = bank[5]
        conv_ps = bank[6]
        tok_ps = [bank[7], bank[6]]
        chain_ps = [bank[5], bank[4]]
        ch_ps = [bank[3], bank[2]]
        logit_ps = [bank[0], bank[1]]
        route_ps = [bank[1], bank[5]]
        pool_ps = [bank[4], bank[7]]
        rep_ps = [bank[0], bank[1]]
        warm_ps = bank[7]

        s = {n: sem(n) for n in (
            "x0_in", "x1_in", "tab0_in", "tab1_in", "woff_in", "wk_in", "qv_in", "ffn_in",
            "warm_set", "hid_set", "eps_set", "pad_set", "gn_var", "gn_std", "pad_done", "gn_done", "off_mm", "off_done",
            "gnt_mm",
            "gnt_done", "offt_mm", "offt_done", "dist_x", "abs_x", "hat_x", "dist_y", "abs_y", "hat_y", "near_n",
            "near_mm", "near_done", "vd_done", "prod", "tr_bank", "evac", "smp_mm", "smp0_done", "smp1_done",
            "s8_done", "conv_mm", "co_mm", "x1_done",
            "lg_mm", "top_done", "prob_done", "route_done", "rt_mm", "rt_done",
            "pl_mm", "pl_done", "sp_mm", "sp_done", "hid_mm", "hid_done", "ex_mm", "ex_done",
            "y_mm", "y_done", "out_done", "vector_op", "act_table")}
        for n in ("ln_mm", "ln_sq", "ln_var", "ln_std", "zt_done", "z_tr", "z_done", "gram_mm", "gram_done",
                  "qg_mm", "qg_done", "part_mm", "part_done", "rep_mm", "rep_done", "step_mm", "step_done",
                  "ga_mm", "ga_done",
                  "move_mm", "move_done", "next_mm", "att_mm", "x2_done"):
            s[n] = [sem(f"{n}{g}") for g in range(G)]

        block = ctx.enter_context(nc.Block())

        def windows(mode, j):
            return (j,) if mode == "local" else (0, NW - 1)

        def hats_of(mode, u):
            size = TAPS * P * len(windows(mode, 0))
            at_u = u % HATS[mode] * size
            return hats[:, at_u:at_u + size]

        def banks(mode, n, j):
            nw = len(windows(mode, 0))
            return n * TAPS * nw * BLOCKS // 4 + -(-TAPS * nw * (j + 1) // 4)

        PN = G * PAIRS
        U = PN * BLOCKS

        @block.sync
        def _(sp):
            sp.dma_start(x_in[0][:], ap["x"][0]).then_inc(s["x0_in"], 16)
            sp.dma_start(table[:, :first_w], ap["table"][:, :first_w]).then_inc(s["tab0_in"], 16)
            sp.dma_start(b_off[:], ap["b_off"]).then_inc(s["woff_in"], 16)
            sp.dma_start(x_in[1][:], ap["x"][1]).then_inc(s["x1_in"], 16)
            sp.dma_start(table[:, first_w:], ap["table"][:, first_w:]).then_inc(s["tab1_in"], 16)
            sp.dma_start(w_k47[:], ap["w_k47"]).then_inc(s["wk_in"], 16)
            sp.dma_start(w_k8[:], ap["w_k8"]).then_inc(s["wk_in"], 16)
            sp.dma_start(q_t[:], ap["q_t"]).then_inc(s["qv_in"], 16)
            sp.dma_start(v_t[:], ap["v_t"]).then_inc(s["qv_in"], 16)
            sp.dma_start(gate_w[:], ap["gate_w"]).then_inc(s["ffn_in"], 16)
            sp.dma_start(gate_b[:], ap["gate_b"]).then_inc(s["ffn_in"], 16)
            sp.dma_start(w1[:], ap["w1"]).then_inc(s["ffn_in"], 16)
            sp.dma_start(b1[:], ap["b1"]).then_inc(s["ffn_in"], 16)
            sp.dma_start(w2[:], ap["w2"]).then_inc(s["ffn_in"], 16)
            sp.dma_start(b2[:], ap["b2"]).then_inc(s["ffn_in"], 16)
            for g in range(G):
                sp.wait_ge(s["y_done"], g + 1)
                sp.dma_start(ap["out"][g], y[g][:]).then_inc(s["out_done"], 16)
            sp.wait_ge(s["out_done"], 16 * G)

        FFN_IN = 16 * 6

        PARTS = ((0, (0,)), (0, (1,)), (1, (0, 1)))

        def part_of(buf, k):
            g, pairs = PARTS[k]
            size = BLOCKS * TAPS * W
            return buf[:, g, pairs[0] * size:(pairs[-1] + 1) * size]

        def distance_x(eng, k):
            g, pairs = PARTS[k]
            n = len(pairs) * BLOCKS
            o = off_t[:, g, pairs[0] * BLOCKS * TAPS:(pairs[-1] + 1) * BLOCKS * TAPS, 1]
            eng.tensor_tensor(
                part_of(hat_x, k).rearrange("p (u n) -> p u n", u=n).rearrange("p u (k q) -> p u k q", k=TAPS),
                at["dx_base"].rearrange("p (k q) -> p k q", k=TAPS).unsqueeze(1).broadcast_to([P, n, TAPS, W]),
                o.rearrange("p (u k) -> p u k", k=TAPS).unsqueeze(3).broadcast_to([P, n, TAPS, W]),
                ALU.add).then_inc(s["dist_x"], 1)

        def distance_y(eng, k):
            g, pairs = PARTS[k]
            n = len(pairs)
            o = off_t[:, g, pairs[0] * BLOCKS * TAPS:(pairs[-1] + 1) * BLOCKS * TAPS, 0]
            eng.tensor_tensor(
                part_of(hat_y, k).rearrange("p (r n) -> p r n", r=n).rearrange("p r (u q) -> p r u q", q=H),
                at["dy_base"].rearrange("p (u q) -> p u q", q=H).unsqueeze(1).broadcast_to([P, n, BLOCKS * TAPS, H]),
                o.rearrange("p (r u) -> p r u", r=n).unsqueeze(3).broadcast_to([P, n, BLOCKS * TAPS, H]),
                ALU.add).then_inc(s["dist_y"], 1)

        @block.gpsimd
        def _(pool):
            pool.memset(warm[:], 0.0).then_inc(s["warm_set"], 1)
            pool.memset(eps[:], EPS).then_inc(s["eps_set"], 1)
            for g in range(G):
                pool.memset(gn_pad[g][:], 0.0).then_inc(s["pad_set"], 1)
            pool.memset(hid_d[:], 0.0).then_inc(s["hid_set"], 1)
            pool.wait_ge(s["tab1_in"], 16)
            pool.wait_ge(s["offt_done"], 1)
            distance_y(pool, 0)
            distance_y(pool, 1)
            pool.wait_ge(s["offt_done"], 2)
            distance_x(pool, 2)
            distance_y(pool, 2)
            pool.wait_ge(s["qv_in"], 32)
            for l in range(LAYERS):
                pool.tensor_tensor(v_d[:, l].rearrange("p h (b c) -> p h b c", b=GB),
                                   v_t[:, l].unsqueeze(2).broadcast_to([P, HEADS, GB, C]),
                                   same_image3.unsqueeze(1).broadcast_to([P, HEADS, GB, C]),
                                   ALU.mult).then_inc(s["vd_done"], 1)

        @block.vector
        def _(dve):
            count = [0]

            def link(ins):
                count[0] += 1
                ins.then_inc(s["vector_op"], 1)
                dve.wait_ge(s["vector_op"], count[0])

            def issue(ins):
                count[0] += 1
                ins.then_inc(s["vector_op"], 1)
                return count[0]

            def inverse_root(v, q, root_done, n, root, tmp, r, final):
                link(dve.reciprocal(q, v))
                dve.wait_ge(root_done, n)
                squared = issue(dve.scalar_tensor_tensor(out=tmp, in0=root, scalar=-0.5, in1=root, op0=ALU.mult,
                                                         op1=ALU.mult))
                issue(dve.tensor_tensor(r, root, q, ALU.mult))
                dve.wait_ge(s["vector_op"], squared)
                link(dve.tensor_tensor(tmp, tmp, q, ALU.mult))
                link(dve.scalar_tensor_tensor(out=final, in0=tmp, scalar=1.5, in1=r, op0=ALU.add, op1=ALU.mult))

            def group_norm(g):
                dve.wait_ge(s["x0_in"] if g == 0 else s["x1_in"], 16)
                link(dve.bn_stats(gn_stats[:, g, :], x_in[g][:]))
                r = gn_r
                dve.bn_aggr(gn_mv[:, g, :], gn_stats[:, g, :]).then_inc(s["gn_var"], 1)
                dve.wait_ge(s["gn_var"], g + 1)
                link(dve.tensor_scalar(r[:, g, 0:1], gn_mv[:, g, 1:2], EPS, None, ALU.add))
                inverse_root(r[:, g, 0:1], r[:, g, 2:3], s["gn_std"], g + 1, r[:, g, 1:2], r[:, g, 3:4], r[:, g, 5:6],
                             r[:, g, 4:5])
                dve.wait_ge(s["pad_set"], g + 1)
                dve.tensor_scalar(gn_pad[g][:, 1:H + 1, 1:W + 1], x_in[g][:].rearrange("p (h w) -> p h w", h=H),
                                  gn_mv[:, g, 0:1], r[:, g, 4:5], ALU.subtract, ALU.mult).then_inc(s["pad_done"], 1)

            def largest(g):
                dve.wait_ge(s["off_done"], g + 1)
                link(dve.tensor_reduce(near_max[:, g:g + 1], off[g][:], AX.X, ALU.max, apply_absolute_value=True))

            def count_near():
                dve.tensor_scalar(near_max[:], near_max[:], 1.0, 0.0, ALU.is_le, ALU.add,
                                  accum_out=near_n[:]).then_inc(s["near_n"], 1)

            def decide():
                dve.wait_ge(s["near_mm"], 1)
                dve.tensor_scalar(is_near[:], bank[6][0:1, 0:1], float(G * GB * TAPS), None,
                                  ALU.is_ge).then_inc(s["near_done"], 1)

            def hat(buf, k, absd, done):
                dve.wait_ge(s[absd], k + 1)
                d = part_of(buf, k)
                dve.tensor_scalar(d, d, 1.0, 1.0, ALU.min, ALU.subtract).then_inc(s[done], 1)

            def product(mode, u):
                nr, g, v = WR if mode == "local" else H, u // UNITS, u % UNITS
                if u in (0, BLOCKS, UNITS):
                    part = (0, BLOCKS, UNITS).index(u)
                    dve.wait_ge(s["hat_x"], part + 1)
                    dve.wait_ge(s["hat_y"], part + 1)
                old = u - HATS[mode]
                if old >= 0:
                    dve.wait_ge(s["tr_bank"], banks(mode, old // BLOCKS, old % BLOCKS))
                r0 = LOCAL_ROWS[v % BLOCKS] if mode == "local" else 0
                hy = hat_y[:, g, v * TAPS * H:(v + 1) * TAPS * H].rearrange("p (k q) -> p k q", k=TAPS)[:, :, r0:r0 + nr]
                hx = hat_x[:, g, v * TAPS * W:(v + 1) * TAPS * W].rearrange("p (k q) -> p k q", k=TAPS)
                out = hats_of(mode, u).rearrange("p (k m) -> p k m", k=TAPS).rearrange("p k (r q) -> p k r q", q=W)
                for taps in ((slice(0, 4), slice(4, TAPS)) if u == 0 else (slice(0, TAPS),)):
                    n = taps.stop - taps.start
                    dve.tensor_tensor(out[:, taps], hy[:, taps].unsqueeze(3).broadcast_to([P, n, nr, W]),
                                      hx[:, taps].unsqueeze(2).broadcast_to([P, n, nr, W]),
                                      ALU.mult).then_inc(s["prod"], 1)

            def sampled(n):
                dve.wait_ge(s["smp_mm"], n + 1)
                if n >= 1:
                    dve.wait_ge(s["conv_mm"], n)
                dve.tensor_copy(samp[:, 0].rearrange("p k t -> p (k t)"), smp_ps[0][:]).then_inc(s["smp0_done"], 1)

            def x1_sum(g):
                dve.wait_ge(s["co_mm"], g + 1)
                dve.tensor_tensor(x1[g][:], conv_ps[:, 0:T], x_in[g][:], ALU.add).then_inc(s["x1_done"], 1)

            def convolve(mode):
                for u in range(U):
                    product(mode, u)
                    n, j = divmod(u, BLOCKS)
                    if j == 2 and n >= 1:
                        sampled(n - 1)
                    if u == 2:
                        hat(hat_x, 1, "abs_x", "hat_x")
                    if u == 3:
                        hat(hat_y, 1, "abs_y", "hat_y")
                    if u == BLOCKS + 1:
                        hat(hat_x, 2, "abs_x", "hat_x")
                    if u == BLOCKS + 3:
                        hat(hat_y, 2, "abs_y", "hat_y")
                    if u == UNITS + 3:
                        x1_sum(0)
                    if u == UNITS + 6:
                        ln_variance(0, 0)
                    if u == UNITS + 7:
                        ln_scale(0, 0)
                gram_start(0)
                sampled(PN - 1)
                x1_sum(G - 1)

            seg = lambda a: a.rearrange("p (s c) -> p s c", c=C)

            def ln_variance(n, g):
                st = lambda k: ln_s[:, n, k, g, :]
                dve.wait_ge(s["ln_sq"][g], n + 1)
                dve.tensor_reduce(st(1), seg(ln_sq[g][:]), AX.X, ALU.add).then_inc(s["ln_var"][g], 1)

            def ln_scale(n, g):
                st = lambda k: ln_s[:, n, k, g, :]
                dve.wait_ge(s["ln_var"][g], n + 1)
                link(dve.tensor_scalar(st(2), st(1), 1.0 / C, EPS, ALU.mult, ALU.add))
                inverse_root(st(2), st(4), s["ln_std"][g], n + 1, st(3), st(5), st(0), st(6))
                dve.tensor_tensor(seg(z_t[n][g][:].rearrange("p h q -> p (h q)")), seg(tok_ps[g][:, 0:T]),
                                  st(6).unsqueeze(2).broadcast_to([P, 2 * GB, C]), ALU.mult).then_inc(s["zt_done"][g], 1)

            def gram_start(g):
                dve.wait_ge(s["gram_mm"][g], 1)
                dve.tensor_tensor(gram[g][:], tok_ps[g][:, 0:P], at["same_image"], ALU.mult).then_inc(s["gram_done"][g], 1)

            def chain_part(l, g):
                dve.wait_ge(s["part_mm"][g], l + 1)
                dve.scalar_tensor_tensor(out=part[g][:], in0=chain_ps[g][:, 0:P], scalar=1.0 / (T * HEADS),
                                         in1=at["first_identity"], op0=ALU.mult, op1=ALU.add).then_inc(s["part_done"][g], 1)

            def chain_step(l, g):
                dve.wait_ge(s["step_mm"][g], l + 1)
                dve.tensor_tensor(step[g][:], chain_ps[g][:, P:2 * P], at["same_image"],
                                  ALU.mult).then_inc(s["step_done"][g], 1)

            def chain_gram(l, g):
                dve.wait_ge(s["ga_mm"][g], l + 1)
                dve.tensor_tensor(ga[g][:], rep_ps[g][:, P:2 * P], at["same_image"],
                                  ALU.mult).then_inc(s["ga_done"][g], 1)

            def chain_next(l, g):
                dve.wait_ge(s["next_mm"][g], l + 1)
                dve.tensor_copy(gram[g][:], chain_ps[g][:, 2 * P:3 * P]).then_inc(s["gram_done"][g], 1)

            def x2_sum(g):
                dve.wait_ge(s["att_mm"][g], 1)
                dve.tensor_tensor(x2[g][:], ch_ps[g][:, 0:T], x1[g][:], ALU.add).then_inc(s["x2_done"][g], 1)

            def experts():
                logit = logit_ps[0][:, 0:T]
                dve.wait_ge(s["lg_mm"], 1)
                dve.max(top[:], logit).then_inc(s["top_done"], 1)
                dve.wait_ge(s["top_done"], 1)
                dve.tensor_scalar(neg_max[:], top[:, 0:1], -1.0, None, ALU.mult).then_inc(s["top_done"], 1)
                link(dve.match_replace(logit_r[:], top[:], logit, -3.0e38))
                issue(dve.tensor_tensor(chosen[:], logit, logit_r[:], ALU.not_equal))
                dve.wait_ge(s["prob_done"], 1)
                link(dve.reciprocal(prob_s[:, 1:2], prob_s[:, 0:1]))
                for h in range(2):
                    q = slice(h * P, (h + 1) * P)
                    dve.scalar_tensor_tensor(out=route[:, q], in0=prob[:, q], scalar=prob_s[:, 1:2], in1=chosen[:, q],
                                             op0=ALU.mult, op1=ALU.mult).then_inc(s["route_done"], 1)
                for g in range(G):
                    dve.wait_ge(s["pl_mm"], g + 1)
                    dve.tensor_tensor(pool_d[:, g], pool_ps[g][:, 0:GB * E], at["image_expert"],
                                      ALU.mult).then_inc(s["pl_done"], 1)
                dve.wait_ge(s["sp_mm"], 1)
                dve.tensor_tensor(pool_e[:].rearrange("p e (g b) -> p g e b", g=G),
                                  bank[5][:, 0:P].rearrange("p (g n) -> p g n", g=G)
                                  .rearrange("p g (e b) -> p g e b", e=E),
                                  at["quarter_expert"].unsqueeze(1).unsqueeze(3).broadcast_to([P, G, E, GB]),
                                  ALU.mult).then_inc(s["sp_done"], 1)
                dve.wait_ge(s["ex_mm"], 1)
                for g in range(G):
                    b = slice(g * GB, (g + 1) * GB)
                    dve.tensor_tensor(ex_d[:, b], bank[7][:, 0:C].unsqueeze(1).broadcast_to([P, GB, C]),
                                      at["own_image"][:, b].unsqueeze(2).broadcast_to([P, GB, C]),
                                      ALU.mult).then_inc(s["ex_done"], 1)
                for g in range(G):
                    dve.wait_ge(s["y_mm"], g + 1)
                    dve.tensor_tensor(y[g][:], ch_ps[g][:, 0:T], x2[g][:], ALU.add).then_inc(s["y_done"], 1)

            for g in range(G):
                group_norm(g)
            dve.wait_ge(s["offt_mm"], 1)
            dve.tensor_copy(off_t[:, 0].rearrange("p u a -> p (u a)"), bank[4][:, 0:UNITS * OC]).then_inc(s["offt_done"], 1)
            dve.wait_ge(s["tab1_in"], 16)
            dve.wait_ge(s["offt_done"], 1)
            distance_x(dve, 0)
            distance_x(dve, 1)
            largest(0)
            hat(hat_x, 0, "abs_x", "hat_x")
            hat(hat_y, 0, "abs_y", "hat_y")
            largest(1)
            count_near()
            decide()
            dve.wait_ge(s["near_done"], 1)
            near_flag = dve.value_load(is_near[0:1, 0:1], min_val=0, max_val=1)
            links = count[0]
            with dve.If(near_flag):
                convolve("local")
            count[0] = links
            with dve.Else():
                convolve("dense")
            chain_part(0, 0)
            chain_step(0, 0)
            chain_gram(0, 0)
            ln_variance(0, 1)
            ln_scale(0, 1)
            gram_start(1)
            chain_part(1, 0)
            for l in range(1, LAYERS):
                chain_step(l, 0)
                if l < LAYERS - 1:
                    chain_gram(l, 0)
                chain_part(l - 1, 1)
                if l == LAYERS - 1:
                    x2_sum(0)
                chain_step(l - 1, 1)
                chain_gram(l - 1, 1)
                chain_next(l - 1, 1)
                if l < LAYERS - 1:
                    chain_part(l + 1, 0)
            ln_variance(1, 0)
            ln_scale(1, 0)
            chain_part(LAYERS - 1, 1)
            chain_step(LAYERS - 1, 1)
            x2_sum(1)
            ln_variance(1, 1)
            ln_scale(1, 1)
            dve.wait_ge(s["ffn_in"], FFN_IN)
            experts()

        @block.scalar
        def _(act):
            act.dma_start(w_off[:], ap["w_off"]).then_inc(s["woff_in"], 16)
            act.wait_ge(s["eps_set"], 1)
            act.activation(prob[:, 0:1], eps[:, 0:1], ACT.Sqrt).then_inc(s["act_table"], 1)

            def group_norm(g):
                act.wait_ge(s["gn_var"], g + 1)
                act.activation(gn_r[:, g, 1:2], gn_mv[:, g, 1:2], ACT.Sqrt, bias=eps[:, 0:1]).then_inc(s["gn_std"], 1)

            def contiguous(g):
                act.wait_ge(s["pad_done"], g + 1)
                act.copy(gn[g][:].rearrange("p (h w) -> p h w", h=H),
                         gn_pad[g][:, 1:H + 1, 1:W + 1]).then_inc(s["gn_done"], 1)

            def offsets(g):
                act.wait_ge(s["off_mm"], g + 1)
                if g == 0:
                    act.wait_ge(s["woff_in"], 32)
                act.activation(off[g][:], bank[g][0:GB * OC, 0:T], ACT.Identity,
                               bias=b_off[0:GB * OC, 0:1]).then_inc(s["off_done"], 1)

            def windows_t(g):
                act.wait_ge(s["gnt_mm"], g + 1)
                act.copy(gn_t[g][:].rearrange("p w q -> p (w q)"), bank[2 + g][:]).then_inc(s["gnt_done"], 1)

            def magnitude(buf, k, dist, absd):
                act.wait_ge(s[dist], k + 1)
                d = part_of(buf, k)
                act.activation(d, d, ACT.Abs).then_inc(s[absd], 1)

            def sampled(n):
                act.wait_ge(s["smp_mm"], n + 1)
                if n >= 1:
                    act.wait_ge(s["conv_mm"], n)
                act.copy(samp[:, 1].rearrange("p k t -> p (k t)"), smp_ps[1][:]).then_inc(s["smp1_done"], 1)
                g, pr = divmod(n, PAIRS)
                if pr == PAIRS - 1:
                    if g:
                        act.wait_ge(s["co_mm"], g)
                    act.copy(samp8[:], s8_ps[:, 0:T]).then_inc(s["s8_done"], 1)

            def convolve(mode):
                nw = len(windows(mode, 0))
                per = TAPS * BLOCKS * nw // 4
                for n in range(PN):
                    if n >= 2:
                        act.wait_ge(s["smp_mm"], n - 1)
                    for i in range(per):
                        if n >= 1 and i == 2 * TAPS * nw // 4:
                            sampled(n - 1)
                        if n == PN - 1 and i == TAPS * nw // 4:
                            ln_square(0, 0)
                        if n == PN - 1 and i == 3 * TAPS * nw // 4:
                            ln_root(0, 0)
                        if n == 0 and i == 3 * TAPS * nw // 4:
                            magnitude(hat_x, 2, "dist_x", "abs_x")
                        if n == 1 and i == 2 * TAPS * nw // 4:
                            magnitude(hat_y, 2, "dist_y", "abs_y")
                        f = n * per + i
                        act.wait_ge(s["tr_bank"], f + 1)
                        act.copy(wts[:, n % 2, 512 * i:512 * i + 512], ring[f % RING][:]).then_inc(s["evac"], 1)
                sampled(PN - 1)

            def ln_square(n, g):
                act.wait_ge(s["ln_mm"][g], n + 1)
                act.activation(ln_sq[g][:], tok_ps[g][:, 0:T], ACT.Square).then_inc(s["ln_sq"][g], 1)

            def ln_root(n, g):
                act.wait_ge(s["ln_var"][g], n + 1)
                act.activation(ln_s[:, n, 3, g, :], ln_s[:, n, 1, g, :], ACT.Sqrt, bias=eps[:, 0:1],
                               scale=1.0 / C).then_inc(s["ln_std"][g], 1)

            def z_copy(n, g):
                act.wait_ge(s["z_tr"][g], n + 1)
                act.copy(z[n][g][:], (ch_ps, tok_ps)[n][g][:, 0:T]).then_inc(s["z_done"][g], 1)

            def chain_heads(l, g):
                act.wait_ge(s["qg_mm"][g], l + 1)
                act.copy(qg[g][:], tok_ps[g][:, 0:HEADS * C]).then_inc(s["qg_done"][g], 1)

            def chain_repeat(l, g):
                act.wait_ge(s["rep_mm"][g], l + 1)
                act.copy(gram_r[g][:], rep_ps[g][:, 0:P]).then_inc(s["rep_done"][g], 1)

            def chain_next(l, g):
                act.wait_ge(s["next_mm"][g], l + 1)
                act.copy(gram[g][:], chain_ps[g][:, 2 * P:3 * P]).then_inc(s["gram_done"][g], 1)

            def chain_move(l, g):
                act.wait_ge(s["move_mm"][g], l + 1)
                act.copy(z[0][g][:], ch_ps[g][:, 0:T]).then_inc(s["move_done"][g], 1)

            for g in range(G):
                group_norm(g)
            for g in range(G):
                contiguous(g)
            offsets(0)
            magnitude(hat_x, 0, "dist_x", "abs_x")
            magnitude(hat_y, 0, "dist_y", "abs_y")
            offsets(1)
            windows_t(0)
            windows_t(1)
            magnitude(hat_x, 1, "dist_x", "abs_x")
            magnitude(hat_y, 1, "dist_y", "abs_y")
            act.wait_ge(s["offt_mm"], 2)
            act.copy(off_t[:, 1].rearrange("p u a -> p (u a)"), bank[5][:, 0:UNITS * OC]).then_inc(s["offt_done"], 1)
            act.wait_ge(s["near_done"], 1)
            near_flag = act.value_load(is_near[0:1, 0:1], min_val=0, max_val=1)
            with act.If(near_flag):
                convolve("local")
            with act.Else():
                convolve("dense")
            chain_heads(0, 0)
            chain_repeat(0, 0)
            z_copy(0, 0)
            ln_square(0, 1)
            ln_root(0, 1)
            chain_next(0, 0)
            chain_move(0, 0)
            chain_heads(1, 0)
            chain_repeat(1, 0)
            z_copy(0, 1)
            for l in range(1, LAYERS):
                chain_heads(l - 1, 1)
                chain_repeat(l - 1, 1)
                if l < LAYERS - 1:
                    chain_next(l, 0)
                if l >= 2:
                    chain_move(l - 2, 1)
                if l < LAYERS - 1:
                    chain_move(l, 0)
                    chain_heads(l + 1, 0)
                if l + 1 < LAYERS - 1:
                    chain_repeat(l + 1, 0)
            ln_square(1, 0)
            ln_root(1, 0)
            chain_heads(LAYERS - 1, 1)
            chain_move(LAYERS - 2, 1)
            z_copy(1, 0)
            ln_square(1, 1)
            ln_root(1, 1)
            act.wait_ge(s["act_table"], 1)
            act.activation(prob[:, 0:1], eps[:, 0:1], ACT.Exp).then_inc(s["act_table"], 1)
            z_copy(1, 1)
            act.wait_ge(s["ffn_in"], FFN_IN)
            act.wait_ge(s["lg_mm"], 2)
            act.wait_ge(s["top_done"], 2)
            act.wait_ge(s["act_table"], 2)
            act.activation(prob[:], logit_ps[1][:, 0:T], ACT.Exp, bias=neg_max[:, 0:1],
                           accum_out=prob_s[:, 0:1]).then_inc(s["prob_done"], 1)
            for h in range(2):
                act.wait_ge(s["rt_mm"], h + 1)
                act.copy(route_t[:, h, :], route_ps[h][:, 0:P]).then_inc(s["rt_done"], 1)
            act.wait_ge(s["hid_mm"], 1)
            act.wait_ge(s["hid_set"], 1)
            act.activation(hid_d[:].rearrange("p q (e n) -> p q e n", e=4)[:, :, :, 0:B],
                           bank[6][:, 0:P].rearrange("p (q e n) -> p q e n", q=4, e=4), ACT.Gelu).then_inc(s["hid_done"], 1)

        @block.tensor
        def _(pe):
            def keep_busy(n):
                pe.wait_ge(s["warm_set"], 1)
                for _ in range(n):
                    pe.matmul(warm_ps[:, 0:T], warm[:, 0:P], warm[:], start=True, stop=True)

            def fill(n, out):
                for _ in range(n):
                    pe.matmul(out[:, 0:P], warm[:, 0:P], warm[:, 0:P], start=True, stop=True)

            def offsets(g, taps):
                pe.wait_ge(s["pad_done"], g + 1)
                if g == 0:
                    pe.wait_ge(s["woff_in"], 32)
                for t in taps:
                    dy, dx = divmod(t, KS)
                    mm = pe.matmul(bank[g][0:GB * OC, 0:T], w_off[:, t, :], gn_pad[g][:, dy:dy + H, dx:dx + W],
                                   start=(t == 0), stop=(t == TAPS - 1))
                if t == TAPS - 1:
                    mm.then_inc(s["off_mm"], 1)

            def windows_t(g):
                pe.wait_ge(s["gn_done"], g + 1)
                for w, r in enumerate(LOCAL_ROWS):
                    mm = pe.transpose(bank[2 + g][:, w * P:(w + 1) * P], gn[g][:, r * W:(r + WR) * W], ident)
                mm.then_inc(s["gnt_mm"], 1)

            def offsets_t(g):
                pe.wait_ge(s["off_done"], g + 1)
                if g == 0:
                    pe.wait_ge(s["tab0_in"], 16)
                out = bank[4 + g][:, 0:UNITS * OC].rearrange("p (r j c) -> p r j c", r=PAIRS, j=BLOCKS)
                pick = at["pick_offsets"][0:GB * OC].rearrange("p (r i c) -> p r i c", r=PAIRS, i=2)
                for j in range(BLOCKS):
                    for i in range(2):
                        mm = pe.matmul(out[i * BP:(i + 1) * BP, :, j, :], off[g][:, j * BP:(j + 1) * BP],
                                       pick[:, :, i, :], start=True, stop=True)
                mm.then_inc(s["offt_mm"], 1)

            def count_near():
                pe.wait_ge(s["tab1_in"], 16)
                pe.wait_ge(s["near_n"], 1)
                pe.matmul(bank[6][0:1, 0:1], near_n[:], at["row_channels"][0:GB * OC, :], start=True,
                          stop=True).then_inc(s["near_mm"], 1)

            def transposes(mode, u, half):
                n, j = divmod(u, BLOCKS)
                nw = len(windows(mode, 0))
                per = TAPS * BLOCKS * nw // 4
                pe.wait_ge(s["prod"], half + 1 if u == 0 else u + 2)
                for i in (range(4 * nw), range(4 * nw, TAPS * nw))[half]:
                    slot = j * TAPS * nw + i
                    f = n * per + slot // 4
                    if slot % 4 == 0 and f >= RING:
                        pe.wait_ge(s["evac"], f - RING + 1)
                    mm = pe.transpose(ring[f % RING][:, (slot % 4) * P:(slot % 4 + 1) * P],
                                      hats_of(mode, u)[:, i * P:(i + 1) * P], ident)
                    if slot % 4 == 3:
                        mm.then_inc(s["tr_bank"], 1)

            def sample(mode, u, i):
                n, j = divmod(u, BLOCKS)
                g, pr = divmod(n, PAIRS)
                nw = len(windows(mode, 0))
                if j == 0 and n:
                    pe.wait_ge(s[f"smp{i}_done"], n)
                if j == 0 and pr == 0 and g:
                    pe.wait_ge(s["s8_done"], g)
                pe.wait_ge(s["evac"], banks(mode, n, j))
                w = wts[:, n % 2, 0:BLOCKS * TAPS * nw * P].rearrange("q (j k m) -> q j k m", j=BLOCKS, k=TAPS)
                w = w.rearrange("q j k (h i p) -> q j k h i p", h=nw, i=2)
                b = 2 * pr + i
                for h, win in enumerate(windows(mode, j)):
                    lhs = gn_t[g][:, win, b * C:(b + 1) * C]
                    for jj in range(4):
                        pe.matmul(
                            smp_ps[i][jj * C:(jj + 1) * C, :].rearrange("p (k t) -> p k t", k=2)[:, :, j * BP:(j + 1) * BP],
                            lhs, w[:, j, jj:TAPS - 1:4, h, i, :], start=(h == 0), stop=(h == nw - 1),
                            tile_position=(0, jj * C))
                    mm = pe.matmul(s8_ps[b * C:(b + 1) * C, j * BP:(j + 1) * BP], lhs, w[:, j, TAPS - 1, h, i, :],
                                   start=(h == 0), stop=(h == nw - 1), tile_position=(0, b * C))
                if j == BLOCKS - 1 and i == 1:
                    mm.then_inc(s["smp_mm"], 1)

            def contract(n):
                g, pr = divmod(n, PAIRS)
                if n == 0:
                    pe.wait_ge(s["wk_in"], 32)
                if pr == 0 and g:
                    pe.wait_ge(s["x1_done"], g)
                pe.wait_ge(s["smp0_done"], n + 1)
                pe.wait_ge(s["smp1_done"], n + 1)
                for k in range(2):
                    for i in range(2):
                        b = 2 * pr + i
                        mm = pe.matmul(conv_ps[b * C:(b + 1) * C, 0:T], w_k47[:, k, :], samp[:, i, k, :],
                                       start=(k == 0), stop=False, tile_position=(0, b * C), skip_group_check=True)
                mm.then_inc(s["conv_mm"], 1)
                if pr == PAIRS - 1:
                    pe.wait_ge(s["s8_done"], g + 1)
                    pe.matmul(conv_ps[:, 0:T], w_k8[:], samp8[:], start=False, stop=True,
                              skip_group_check=True).then_inc(s["co_mm"], 1)

            def convolve(mode):
                pe.wait_ge(s["gnt_done"], G)
                for u in range(U):
                    transposes(mode, u, 0)
                    transposes(mode, u, 1)
                    if u > BLOCKS and u % BLOCKS == 2:
                        contract(u // BLOCKS - 1)
                    if u >= 2:
                        sample(mode, u - 2, 0)
                        sample(mode, u - 2, 1)
                    if u == UNITS + 3:
                        center(0, 0)
                for u in range(U - 2, U):
                    for i in range(2):
                        sample(mode, u, i)
                    if u == U - 2:
                        gram_start(0)
                pe.wait_ge(s["qv_in"], 32)
                chain_heads(0, 0)
                chain_repeat(0, 0)
                contract(PN - 1)

            def center(n, g):
                src = (x1, x2)[n]
                if n == 0:
                    pe.wait_ge(s["x1_done"], g + 1)
                else:
                    pe.wait_ge(s["x2_done"][g], 1)
                for h in range(2):
                    mm = pe.matmul(tok_ps[g][:, h * P:(h + 1) * P], src[g][:, h * P:(h + 1) * P], at["center"],
                                   start=True, stop=True)
                mm.then_inc(s["ln_mm"][g], 1)

            def gram_start(g):
                pe.wait_ge(s["zt_done"][g], 1)
                for h in range(2):
                    mm = pe.matmul(tok_ps[g][:, 0:P], z_t[0][g][:, h, :], z_t[0][g][:, h, :], start=(h == 0), stop=(h == 1))
                mm.then_inc(s["gram_mm"][g], 1)

            def z_back(n, g):
                pe.wait_ge(s["zt_done"][g], n + 1)
                for h in range(2):
                    mm = pe.transpose((ch_ps, tok_ps)[n][g][:, h * P:(h + 1) * P], z_t[n][g][:, h, :], ident)
                mm.then_inc(s["z_tr"][g], 1)

            def chain_heads(l, g):
                pe.wait_ge(s["gram_done"][g], l + 1)
                pe.matmul(tok_ps[g][:, 0:HEADS * C], gram[g][:], q_t[:, l, :], start=True, stop=True).then_inc(s["qg_mm"][g], 1)

            def chain_part(l, g):
                pe.wait_ge(s["qg_done"][g], l + 1)
                pe.wait_ge(s["vd_done"], l + 1)
                for k in range(HEADS // 4):
                    for r in range(4):
                        h = 4 * k + r
                        mm = pe.matmul(chain_ps[g][r * C:(r + 1) * C, 0:P], qg[g][:, h * C:(h + 1) * C], v_d[:, l, h, :],
                                       start=(k == 0), stop=(k == HEADS // 4 - 1), tile_position=(0, r * C),
                                       skip_group_check=True)
                mm.then_inc(s["part_mm"][g], 1)

            def chain_step(l, g):
                pe.wait_ge(s["part_done"][g], l + 1)
                pe.matmul(chain_ps[g][:, P:2 * P], at["spread"], part[g][:], start=True, stop=True).then_inc(s["step_mm"][g], 1)

            def chain_repeat(l, g):
                pe.matmul(rep_ps[g][:, 0:P], at["spread"], gram[g][:], start=True, stop=True).then_inc(s["rep_mm"][g], 1)

            def chain_gram(l, g):
                pe.wait_ge(s["rep_done"][g], l + 1)
                pe.matmul(rep_ps[g][:, P:2 * P], gram_r[g][:], part[g][:], start=True,
                          stop=True).then_inc(s["ga_mm"][g], 1)

            def chain_move(l, g, half):
                pe.wait_ge(s["step_done"][g], l + 1)
                if l:
                    pe.wait_ge(s["move_done"][g], l)
                else:
                    pe.wait_ge(s["z_done"][g], 1)
                q = slice(half * P, (half + 1) * P)
                mm = pe.matmul(ch_ps[g][:, q], step[g][:], z[0][g][:, q], start=True, stop=True)
                if half == 1:
                    mm.then_inc(s["move_mm"][g], 1)

            def chain_next(l, g):
                pe.wait_ge(s["step_done"][g], l + 1)
                pe.wait_ge(s["ga_done"][g], l + 1)
                pe.matmul(chain_ps[g][:, 2 * P:3 * P], step[g][:], ga[g][:], start=True, stop=True).then_inc(s["next_mm"][g], 1)

            def attend(g):
                pe.wait_ge(s["step_done"][g], LAYERS)
                pe.wait_ge(s["move_done"][g], LAYERS - 1)
                pe.matmul(ch_ps[g][:, 0:T], step[g][:], z[0][g][:], start=True, stop=True).then_inc(s["att_mm"][g], 1)

            def gate_start():
                pe.wait_ge(s["ffn_in"], FFN_IN)
                pe.wait_ge(s["z_done"][0], 2)
                for m in range(2):
                    pe.matmul(logit_ps[m][:, 0:T], at["expert_columns"][0:E, :], gate_b[:], start=True, stop=False)
                    pe.matmul(logit_ps[m][:, 0:T], gate_w[:, 0, :], z[1][0][:], start=False, stop=False)

            def experts():
                pe.wait_ge(s["z_done"][1], 2)
                for m in range(2):
                    pe.matmul(logit_ps[m][:, 0:T], gate_w[:, 1, :], z[1][1][:], start=False,
                              stop=True).then_inc(s["lg_mm"], 1)
                fill(8, bank[3])
                for h in range(2):
                    pe.wait_ge(s["route_done"], h + 1)
                    pe.transpose(route_ps[h][:, 0:P], route[:, h * P:(h + 1) * P], ident).then_inc(s["rt_mm"], 1)
                pe.matmul(bank[6][:, 0:P], b1[:], at["expert_columns"][0:E, :], start=True, stop=False,
                          skip_group_check=True)
                for h in range(2):
                    pe.wait_ge(s["rt_done"], h + 1)
                    for g in range(G):
                        mm = pe.matmul(pool_ps[g][:, 0:GB * E], z_t[1][g][:, h, :],
                                       route_t[:, h, :].rearrange("p (e i) -> p e i", e=E)[:, :, g * GB:(g + 1) * GB],
                                       start=(h == 0), stop=(h == 1))
                        if h == 1:
                            mm.then_inc(s["pl_mm"], 1)
                fill(2, bank[0])
                pe.wait_ge(s["pl_done"], G)
                pe.matmul(bank[5][:, 0:P], at["spread"], pool_d[:].rearrange("p g q -> p (g q)"), start=True,
                          stop=True).then_inc(s["sp_mm"], 1)
                fill(2, bank[0])
                pe.wait_ge(s["sp_done"], 1)
                for j in range(E // 4):
                    mm = pe.matmul(bank[6][:, 4 * B * j:4 * B * (j + 1)], w1[:, j, :],
                                   pool_e[:, 4 * j:4 * j + 4, :].rearrange("p e i -> p (e i)"), start=False,
                                   stop=(j == E // 4 - 1), skip_group_check=True)
                mm.then_inc(s["hid_mm"], 1)
                pe.matmul(bank[7][:, 0:C], at["expert_columns"][0:E, :], b2[:], start=True, stop=False,
                          skip_group_check=True)
                pe.wait_ge(s["hid_done"], 1)
                for e in range(4):
                    for q in range(4):
                        mm = pe.matmul(bank[7][q * 4 * B:(q + 1) * 4 * B, 0:C], hid_d[:, q, e * 4 * B:(e + 1) * 4 * B],
                                       w2[:, 4 * q + e, :], start=False, stop=(e == 3),
                                       tile_position=(0, q * 4 * B), skip_group_check=True)
                mm.then_inc(s["ex_mm"], 1)
                fill(2, bank[0])
                for g in range(G):
                    pe.wait_ge(s["ex_done"], g + 1)
                    pe.wait_ge(s["x2_done"][g], 1)
                    pe.matmul(ch_ps[g][:, 0:T], ex_d[:, g * GB:(g + 1) * GB, :].rearrange("p b o -> p (b o)"), route[:],
                              start=True, stop=True).then_inc(s["y_mm"], 1)

            keep_busy(5)
            offsets(0, range(TAPS))
            offsets(1, range(KS))
            offsets_t(0)
            offsets(1, range(KS, TAPS))
            windows_t(0)
            windows_t(1)
            count_near()
            offsets_t(1)
            keep_busy(1)
            pe.wait_ge(s["near_done"], 1)
            near_flag = pe.value_load(is_near[0:1, 0:1], min_val=0, max_val=1)
            with pe.If(near_flag):
                convolve("local")
            with pe.Else():
                convolve("dense")
            z_back(0, 0)
            chain_part(0, 0)
            center(0, 1)
            chain_step(0, 0)
            chain_gram(0, 0)
            chain_move(0, 0, 0)
            chain_next(0, 0)
            chain_move(0, 0, 1)
            chain_heads(1, 0)
            chain_repeat(1, 0)
            gram_start(1)
            chain_part(1, 0)
            z_back(0, 1)
            for l in range(1, LAYERS):
                chain_heads(l - 1, 1)
                chain_repeat(l - 1, 1)
                chain_step(l, 0)
                if l < LAYERS - 1:
                    chain_gram(l, 0)
                if l >= 2:
                    chain_move(l - 2, 1, 0)
                chain_part(l - 1, 1)
                if l < LAYERS - 1:
                    chain_next(l, 0)
                    chain_move(l, 0, 0)
                else:
                    attend(0)
                if l >= 2:
                    chain_move(l - 2, 1, 1)
                chain_step(l - 1, 1)
                chain_gram(l - 1, 1)
                if l < LAYERS - 1:
                    chain_move(l, 0, 1)
                    chain_heads(l + 1, 0)
                if l + 1 < LAYERS - 1:
                    chain_repeat(l + 1, 0)
                if l == LAYERS - 1:
                    center(1, 0)
                chain_next(l - 1, 1)
                if l < LAYERS - 1:
                    chain_part(l + 1, 0)
            chain_heads(LAYERS - 1, 1)
            chain_move(LAYERS - 2, 1, 0)
            chain_move(LAYERS - 2, 1, 1)
            chain_part(LAYERS - 1, 1)
            z_back(1, 0)
            chain_step(LAYERS - 1, 1)
            attend(1)
            center(1, 1)
            gate_start()
            z_back(1, 1)
            experts()


def kernel(x, L0_conv_w_off, L0_conv_b_off, L0_conv_w_dcn, L1_attn_v_matrix, L1_attn_q_matrix,
           L1_ffn_gate_w, L1_ffn_gate_b, L1_ffn_weight1, L1_ffn_weight2):
    import concourse.bacc as bacc
    from concourse.bass_utils import run_bass_kernel_spmd

    f = np.float32
    consts = constants()
    names = list(FIRST) + [n for n in consts if n not in FIRST]
    a = {"table": np.concatenate([consts[n] for n in names], axis=1)}
    a["x"] = np.asarray(x).reshape(G, P, T)

    wo = np.asarray(L0_conv_w_off).reshape(OC, C, TAPS).transpose(1, 2, 0)
    w = np.zeros((GB, C, TAPS, GB, OC), f)
    for b in range(GB):
        w[b, :, :, b] = wo
    a["w_off"] = w.reshape(P, TAPS, GB * OC)
    a["b_off"] = np.zeros((P, 1), f)
    a["b_off"][:GB * OC, 0] = np.tile(np.asarray(L0_conv_b_off), GB)

    wd = np.asarray(L0_conv_w_dcn).reshape(C, C, TAPS).transpose(2, 1, 0)
    a["w_k47"] = np.ascontiguousarray(wd[:8].reshape(2, P, C).transpose(1, 0, 2))
    w8 = np.zeros((GB, C, GB, C), f)
    for b in range(GB):
        w8[b, :, b] = wd[8]
    a["w_k8"] = w8.reshape(P, P)

    q = np.asarray(L1_attn_q_matrix)[:, :, 0].transpose(3, 0, 1, 2).reshape(C, LAYERS, HEADS * C)
    a["q_t"] = np.tile(q, (GB, 1, 1))
    v = np.asarray(L1_attn_v_matrix)[:, :, 0].transpose(3, 0, 1, 2)
    a["v_t"] = np.tile(v, (GB, 1, 1, 1))

    gw = np.zeros((GB, C, G, E, B), f)
    for g in range(G):
        for b in range(GB):
            gw[b, :, g, :, g * GB + b] = np.asarray(L1_ffn_gate_w).T
    a["gate_w"] = gw.reshape(P, G, P)
    a["gate_b"] = np.repeat(np.asarray(L1_ffn_gate_b)[:, None], T, axis=1)
    w1, w2 = np.asarray(L1_ffn_weight1), np.asarray(L1_ffn_weight2)
    a["w1"] = np.ascontiguousarray(w1[:, :C].reshape(E // 4, P, HID).transpose(1, 0, 2))
    a["b1"] = np.ascontiguousarray(w1[:, C])
    a["w2"] = np.ascontiguousarray(w2[:, :HID].transpose(1, 0, 2))
    a["b2"] = np.ascontiguousarray(w2[:, HID])

    nc = bacc.Bacc("TRN2", target_bir_lowering=False, num_devices=1)
    ap = {n: nc.dram_tensor("in_" + n, v.shape, F32, kind="ExternalInput").ap() for n, v in a.items()}
    ap["out"] = nc.dram_tensor("out", (G, P, T), F32, kind="ExternalOutput").ap()
    build(nc, ap)
    r = run_bass_kernel_spmd(nc, [{"in_" + n: v for n, v in a.items()}], core_ids=[0])
    return r.results[0]["out"].reshape(B, C, H, W)
```
